# Optimizing a Trainium2 kernel written in Bass

```python
import numpy as np
import jax
import jax.numpy as jnp

def _softmax(x, axis=-1):
    return jax.nn.softmax(x, axis=axis)

def _gelu(x):
    return jax.nn.gelu(x, approximate=True)

def _silu(x):
    return jax.nn.silu(x)

def _sigmoid(x):
    return jax.nn.sigmoid(x)

def _layernorm(x, axis=-1, eps=1e-05):
    m = jnp.mean(x, axis=axis, keepdims=True)
    v = jnp.var(x, axis=axis, keepdims=True)
    return (x - m) / jnp.sqrt(v + eps)

def _scatter_add(tgt, idx, src, axis=0):
    return tgt.at[idx].add(src)

def _segment_sum(src, seg, n):
    return jax.ops.segment_sum(src, seg, n)
kernel_name = 'mk_lm_tower_d1_tok_ids768_r4_19dda6'

def setup_inputs(seed: int=0):
    np.random.seed(seed)
    _w = jnp.asarray

    def _rec_inputs():
        import jax
        import jax.numpy as jnp
        _rk = jax.random.key(seed)
        x = jax.random.randint(jax.random.fold_in(_rk, 1), (8, 256), 0, 12565, jnp.int32)
        return x
    x = _rec_inputs()

    def _L0_tok_setup():
        import jax, jax.numpy as jnp
        import numpy as np
        VOCAB, RANK, D_MODEL = (12565, 64, 192)
        B, S = (8, 1024)
        key = jax.random.key(seed)
        k_ids, k_emb, k_proj = jax.random.split(key, 3)
        input_ids = jax.random.randint(k_ids, (B, S), 0, VOCAB)
        embed_table = jax.random.normal(k_emb, (VOCAB, RANK), dtype=jnp.float32) * 0.02
        proj_up = jax.random.normal(k_proj, (D_MODEL, RANK), dtype=jnp.float32) * 0.02
        return {'input_ids': input_ids, 'embed_table': embed_table, 'proj_up': proj_up}
    _L0_tok_all = _L0_tok_setup()
    _L0_tok_in = {k: v for k, v in _L0_tok_all.items() if k in ('embed_table', 'proj_up')}
    del _L0_tok_all

    def _L0_attn_setup():
        import jax, jax.numpy as jnp
        import numpy as np
        import math
        B, S, D = (4, 1024, 192)
        key = jax.random.key(seed)
        ks = jax.random.split(key, 7)
        sc = 0.02
        return {'x': jax.random.normal(ks[0], (B, S, D), dtype=jnp.float32), 'Wq': jax.random.normal(ks[1], (D, D), dtype=jnp.float32) * sc, 'bq': jax.random.normal(ks[2], (D,), dtype=jnp.float32) * sc, 'Wk': jax.random.normal(ks[3], (D, D), dtype=jnp.float32) * sc, 'bk': jax.random.normal(ks[4], (D,), dtype=jnp.float32) * sc, 'Wv': jax.random.normal(ks[5], (D, D), dtype=jnp.float32) * sc, 'bv': jax.random.normal(ks[6], (D,), dtype=jnp.float32) * sc}
    _L0_attn_all = _L0_attn_setup()
    _L0_attn_in = {k: v for k, v in _L0_attn_all.items() if k in ('Wq', 'bq', 'Wk', 'bk', 'Wv', 'bv')}
    del _L0_attn_all

    def _L0_ffn_setup():
        import jax, jax.numpy as jnp
        import numpy as np
        D = 192
        H = 768
        G = 4
        E = 4
        KG = 2
        KE = 1
        EPS = 1e-05
        key = jax.random.key(seed)
        ks = jax.random.split(key, 12)
        s = 0.02
        x = jax.random.normal(ks[0], (2, 256, D), dtype=jnp.float32)
        Wg = jax.random.normal(ks[1], (D, G), dtype=jnp.float32) * s
        bg = jnp.zeros((G,), jnp.float32)
        We = jax.random.normal(ks[2], (G, D, E), dtype=jnp.float32) * s
        be = jnp.zeros((G, E), jnp.float32)
        W1 = jax.random.normal(ks[3], (G, E, D, H), dtype=jnp.float32) * s
        b1 = jnp.zeros((G, E, H), jnp.float32)
        W2 = jax.random.normal(ks[4], (G, E, H, D), dtype=jnp.float32) * s
        b2 = jnp.zeros((G, E, D), jnp.float32)
        Wp = jax.random.normal(ks[5], (D, D), dtype=jnp.float32) * s
        bp = jnp.zeros((D,), jnp.float32)
        gamma = jnp.ones((D,), jnp.float32)
        beta = jnp.zeros((D,), jnp.float32)
        return {'x': x, 'Wg': Wg, 'bg': bg, 'We': We, 'be': be, 'W1': W1, 'b1': b1, 'W2': W2, 'b2': b2, 'Wp': Wp, 'bp': bp, 'gamma': gamma, 'beta': beta}
    _L0_ffn_all = _L0_ffn_setup()
    _L0_ffn_in = {k: v for k, v in _L0_ffn_all.items() if k in ('Wg', 'bg', 'We', 'be', 'W1', 'b1', 'W2', 'b2', 'Wp', 'bp', 'gamma', 'beta')}
    del _L0_ffn_all
    return {'x': x, 'L0_tok_embed_table': _L0_tok_in['embed_table'], 'L0_tok_proj_up': _L0_tok_in['proj_up'], 'L0_attn_Wq': _L0_attn_in['Wq'], 'L0_attn_bq': _L0_attn_in['bq'], 'L0_attn_Wk': _L0_attn_in['Wk'], 'L0_attn_bk': _L0_attn_in['bk'], 'L0_attn_Wv': _L0_attn_in['Wv'], 'L0_attn_bv': _L0_attn_in['bv'], 'L0_ffn_Wg': _L0_ffn_in['Wg'], 'L0_ffn_bg': _L0_ffn_in['bg'], 'L0_ffn_We': _L0_ffn_in['We'], 'L0_ffn_be': _L0_ffn_in['be'], 'L0_ffn_W1': _L0_ffn_in['W1'], 'L0_ffn_b1': _L0_ffn_in['b1'], 'L0_ffn_W2': _L0_ffn_in['W2'], 'L0_ffn_b2': _L0_ffn_in['b2'], 'L0_ffn_Wp': _L0_ffn_in['Wp'], 'L0_ffn_bp': _L0_ffn_in['bp'], 'L0_ffn_gamma': _L0_ffn_in['gamma'], 'L0_ffn_beta': _L0_ffn_in['beta']}

def reference(x, L0_tok_embed_table, L0_tok_proj_up, L0_attn_Wq, L0_attn_bq, L0_attn_Wk, L0_attn_bk, L0_attn_Wv, L0_attn_bv, L0_ffn_Wg, L0_ffn_bg, L0_ffn_We, L0_ffn_be, L0_ffn_W1, L0_ffn_b1, L0_ffn_W2, L0_ffn_b2, L0_ffn_Wp, L0_ffn_bp, L0_ffn_gamma, L0_ffn_beta):
    import jax
    import jax.numpy as jnp

    def _L0_tok_ref(input_ids, embed_table, proj_up):
        import jax, jax.numpy as jnp
        import numpy as np
        VOCAB, RANK, D_MODEL = (12565, 64, 192)
        B, S = (8, 1024)
        low = embed_table[input_ids]
        return jnp.einsum('bsr,dr->bsd', low, proj_up)

    def _L0_attn_ref(x, Wq, bq, Wk, bk, Wv, bv):
        import jax, jax.numpy as jnp
        import numpy as np
        import math
        B, S, D = (4, 1024, 192)
        q = jnp.einsum('bsd,ed->bse', x, Wq) + bq
        k = jnp.einsum('bsd,ed->bse', x, Wk) + bk
        v = jnp.einsum('bsd,ed->bse', x, Wv) + bv
        scale = 1.0 / math.sqrt(x.shape[-1])
        scores = jnp.einsum('bsd,btd->bst', q, k) * scale
        return jnp.einsum('bst,btd->bsd', scores, v)

    def _L0_ffn_ref(x, Wg, bg, We, be, W1, b1, W2, b2, Wp, bp, gamma, beta):
        import jax, jax.numpy as jnp
        import numpy as np
        D = 192
        H = 768
        G = 4
        E = 4
        KG = 2
        KE = 1
        EPS = 1e-05
        pg = jax.nn.softmax(jnp.einsum('bsd,dg->bsg', x, Wg) + bg, axis=-1)
        gw, gi = jax.lax.top_k(pg, KG)
        pe = jax.nn.softmax(jnp.einsum('bsd,gde->bsge', x, We) + be, axis=-1)
        ew, ei = jax.lax.top_k(pe, KE)
        h = jax.nn.gelu(jnp.einsum('bsd,gedh->bsgeh', x, W1) + b1, approximate=False)
        oe = jnp.einsum('bsgeh,gehf->bsgef', h, W2) + b2
        sel = jnp.take_along_axis(oe, ei[..., None], axis=3)
        grp = jnp.sum(sel * ew[..., None], axis=3)
        gsel = jnp.take_along_axis(grp, gi[..., None], axis=2)
        out = jnp.sum(gsel * gw[..., None], axis=2)
        y = jnp.einsum('bsd,df->bsf', out, Wp) + bp
        mu = jnp.mean(y, axis=-1, keepdims=True)
        var = jnp.mean(jnp.square(y - mu), axis=-1, keepdims=True)
        return (y - mu) * jax.lax.rsqrt(var + EPS) * gamma + beta
    h = _L0_tok_ref(x, L0_tok_embed_table, L0_tok_proj_up)
    h = h + _L0_attn_ref(_layernorm(h, axis=-1), L0_attn_Wq, L0_attn_bq, L0_attn_Wk, L0_attn_bk, L0_attn_Wv, L0_attn_bv)
    h = h + _L0_ffn_ref(_layernorm(h, axis=-1), L0_ffn_Wg, L0_ffn_bg, L0_ffn_We, L0_ffn_be, L0_ffn_W1, L0_ffn_b1, L0_ffn_W2, L0_ffn_b2, L0_ffn_Wp, L0_ffn_bp, L0_ffn_gamma, L0_ffn_beta)
    return h

_drawn_inputs = setup_inputs


def setup_inputs(seed=0):
    import zlib

    import numpy as np

    out = dict(_drawn_inputs(seed))
    spreads = {'L0_ffn_bg': (0.0, 0.8),
     'L0_ffn_be': (0.0, 0.302),
     'L0_ffn_b1': (0.0, 0.703),
     'L0_ffn_b2': (0.0, 0.1),
     'L0_ffn_bp': (0.0, 0.1),
     'L0_ffn_gamma': (1.0, 0.2),
     'L0_ffn_beta': (0.0, 0.1)}
    factors = {}
    for name, (base, spread) in spreads.items():
        noise = np.random.default_rng([zlib.crc32(name.encode()), seed]).standard_normal(out[name].shape)
        drawn = base * np.exp(spread * noise) if base else spread * noise
        out[name] = jnp.asarray(drawn.astype(out[name].dtype))
    for name, factor in factors.items():
        out[name] = (out[name] * factor).astype(out[name].dtype)
    return out
```

```python
from contextlib import ExitStack

import numpy as np

import concourse.bass as bass
from concourse import mybir

F32 = mybir.dt.float32
F16 = mybir.dt.float16
BF16 = mybir.dt.bfloat16
I32 = mybir.dt.int32
U32 = mybir.dt.uint32
ALU = mybir.AluOpType
ACT = mybir.ActivationFunctionType
AX = mybir.AxisListType

P = 128
EPS = 1e-5


def at_least(eng, sem, count):
    if isinstance(count, int) and count <= 0:
        return
    eng.wait_ge(sem, count)


def lm_tower(nc, x, table, proj, Wq, bq, Wk, bk, Wv, bv, Wg, bg, We, be, W1, b1, W2, b2, Wp, bp, gamma, beta, out):
    B, S = x.shape
    VOCAB, RANK = table.shape
    D = proj.shape[0]
    G, E = We.shape[0], We.shape[2]
    H = W1.shape[3]
    NT = B * S // P
    TOKENS = NT * P
    CB = S // P
    DR = D - P
    D1 = D + 1
    EX = G * E
    K = 2
    HC = H // P
    C = 1 + G
    SLOTS = 4
    ROUNDS = -(-(K * TOKENS // P + EX - 1) // SLOTS)
    ST = ROUNDS * SLOTS
    STP = ST + SLOTS
    assert (CB, RANK, K) == (2, 64, 2) and HC * P == H and S == CB * P

    ROW = 200
    x_rows = nc.dram_tensor("x_rows", [TOKENS, ROW], F32).ap()
    y_rows = nc.dram_tensor("y_rows", [K * TOKENS + SLOTS * P, D], F32).ap()

    with ExitStack() as ctx:
        def sb(name, shape, dt=F32):
            return ctx.enter_context(nc.sbuf_tensor(name, shape, dt))

        def sem(name):
            return ctx.enter_context(nc.semaphore(name))

        diff = sb("diff", [P, P])
        ident = sb("ident", [P, P])
        before = sb("before", [P, P], BF16)
        ones = sb("ones", [P, P], BF16)
        lane = sb("lane", [P, P], F16)
        rank4 = sb("rank4", [P, G])
        step128 = sb("step128", [P, NT])
        tile_no = sb("tile_no", [P, STP])
        carry = sb("carry", [P, EX, NT])
        row_id = sb("row_id", [P, K, NT])
        dump = sb("dump", [P, STP // SLOTS, SLOTS])
        ids = sb("ids", [P, NT], I32)
        proj_m = sb("proj_m", [P, 2, RANK])
        proj_r = sb("proj_r", [DR, 2, RANK])
        projT = sb("projT", [P, D])
        qkv_m = sb("qkv_m", [P, 3, D1])
        qkv_r = sb("qkv_r", [DR, 3, D1])
        AT_m = sb("AT_m", [P, D1])
        AT_r = sb("AT_r", [DR + 1, D1])
        WvT_m = sb("WvT_m", [P, D])
        WvT_r = sb("WvT_r", [DR + 1, D])
        gate_m = sb("gate_m", [P, C, 4])
        gate_r = sb("gate_r", [DR, C, 4])
        gate_b = sb("gate_b", [P, C, 4])
        Wp_m = sb("Wp_m", [P, D])
        Wp_r = sb("Wp_r", [DR + EX + 1, D])
        b2_s = sb("b2_s", [EX, D])
        b2T_m = sb("b2T_m", [P, EX])
        b2T_r = sb("b2T_r", [DR, EX])
        b2p = sb("b2p", [EX, D])
        gam = sb("gam", [P, D])
        bet = sb("bet", [P, D])
        emb = sb("emb", [P, NT, RANK])
        lowT = sb("lowT", [P, 2, P])
        h = sb("h", [P, NT, D])
        h2 = sb("h2", [P, NT, D])
        xh = sb("xh", [P, 2, CB, D1])
        xT_m = sb("xT_m", [P, 2, CB * P])
        xT_r = sb("xT_r", [DR + 1, 2, CB * P])
        gram_m = sb("gram_m", [P, 2, D1])
        gram_r = sb("gram_r", [DR + 1, 2, D1])
        gv_m = sb("gv_m", [P, 2, D])
        gv_r = sb("gv_r", [DR + 1, 2, D])
        bb_m = sb("bb_m", [P, 2, D])
        bb_r = sb("bb_r", [DR + 1, 2, D])
        x2 = sb("x2", [P, NT, ROW])
        x2T_m = sb("x2T_m", [P, 2, CB * P])
        x2T_r = sb("x2T_r", [DR, 2, CB * P])
        stats = sb("stats", [P, 2, CB, 6])
        mv = sb("mv", [P, 3, CB, 2])
        ve = sb("ve", [P, 3, CB])
        sd = sb("sd", [P, 3, CB])
        rs = sb("rs", [P, 3, CB])
        tn = sb("tn", [P, 3, CB])
        lg = sb("lg", [P, NT * C, 4])
        lx = sb("lx", [P, NT * C, 4])
        r4 = sb("r4", [P, NT * C])
        pr = sb("pr", [P, NT, C, 4])
        pmax = sb("pmax", [P, NT, C])
        first = sb("first", [P, NT, C, 4])
        key = sb("key", [P, NT * C, 4])
        kmax = sb("kmax", [P, NT * C])
        pg2 = sb("pg2", [P, NT, G])
        second = sb("second", [P, NT, G])
        gmax2 = sb("gmax2", [P, NT])
        sel = sb("sel", [P, K, NT, EX])
        both = sb("both", [P, NT, EX], BF16)
        wg_ = sb("wg_", [P, NT, G])
        wk = sb("wk", [P, K, NT])
        total = sb("total", [P, EX, NT])
        upto = sb("upto", [P, EX, NT])
        more = sb("more", [P, EX, NT])
        tiles_e = sb("tiles_e", [P, EX])
        end_e = sb("end_e", [P, EX])
        unit = sb("unit", [P, EX])
        base_e = sb("base_e", [P, EX])
        past = sb("past", [1, STP, EX])
        expert_f = sb("expert_f", [1, STP])
        expert = sb("expert", [1, STP], I32)
        place = sb("place", [P, NT, EX])
        placed = sb("placed", [P, K, NT, EX])
        slot_f = sb("slot_f", [P, K * NT])
        slot_i = sb("slot_i", [P, K * NT], I32)
        slot_t = sb("slot_t", [P, 2, K * NT], I32)
        slot_p = sb("slot_p", [P, 2, K * NT])
        inv = sb("inv", [P, 6, STP])
        token_of = sb("token_of", [P, STP], I32)
        dest_of = sb("dest_of", [P, STP], I32)
        mixw = sb("mixw", [P, NT, D + EX + 1])
        wsel = sb("wsel", [P, NT, EX])
        token_i = [sb(f"token_i{u}", [P, 1], I32) for u in range(SLOTS)]
        dest_i = [sb(f"dest_i{u}", [P, 1], I32) for u in range(SLOTS)]
        xg = [sb(f"xg{u}", [P, ROW]) for u in range(SLOTS)]
        xs_m = [sb(f"xs_m{u}", [P, P]) for u in range(2)]
        xs_r = [sb(f"xs_r{u}", [DR + 1, P]) for u in range(2)]
        W1_m = [sb(f"W1_m{u}", [P, H]) for u in range(SLOTS)]
        W1_r = [sb(f"W1_r{u}", [DR + 1, H]) for u in range(SLOTS)]
        W2_s = [sb(f"W2_s{u}", [P, HC, D]) for u in range(SLOTS)]
        hT = [sb(f"hT{u}", [P, H]) for u in range(2)]
        yo = [sb(f"yo{u}", [P, D]) for u in range(SLOTS)]
        ys = sb("ys", [P, K, NT, D])
        room = ys[:, 0, :, :].rearrange("p i d -> p (i d)").bitcast(F16)
        hot_lane = room[:, 0:K * NT * P].rearrange("p (m l) -> p m l", l=P)
        hot_tile = room[:, K * NT * P:K * NT * (P + ST)].rearrange("p (m t) -> p m t", t=ST)
        mixT_m = sb("mixT_m", [P, 2, P])
        mixT_r = sb("mixT_r", [DR + EX + 1, 2, P])
        fin = h

        pA = [ctx.enter_context(nc.psum_tensor(f"pA{u}", [P, 1024], F32)) for u in range(2)]
        pX = [ctx.enter_context(nc.psum_tensor(f"pX{u}", [P, 512], F32)) for u in range(2)]
        pY = [ctx.enter_context(nc.psum_tensor(f"pY{u}", [P, 512], F32)) for u in range(2)]
        ps_low = pA[0][:, 0:P]
        ps_lg = pA[0][:, P:P + NT * C * 4]
        ps_h = [pA[0][:, 512:512 + D], pA[1][:, 0:D]]
        ps_xm = pA[1][:, 512:512 + CB * P]
        ps_xr = pA[1][0:DR + 1, 512 + CB * P:1024]
        ps_x2m, ps_x2r = ps_xm, ps_xr[0:DR, :]
        ps_gm, ps_gr = pX[0][:, 0:D1], pX[0][0:DR + 1, D1:2 * D1]
        ps_vm, ps_vr = pX[1][:, 0:D], pX[1][0:DR + 1, D:2 * D]
        ps_bm, ps_br = pY[0][:, 0:D], pY[0][0:DR + 1, D:2 * D]
        ps_o = pY[1][:, 0:CB * D].rearrange("p (c d) -> p c d", c=CB)
        ps_am, ps_ar = pX[0][:, 0:D1], pX[0][0:DR + 1, D1:2 * D1]
        ps_wm, ps_wr = pX[1][:, 0:D], pX[1][0:DR + 1, D:2 * D]
        ps_pr = pY[0][:, 0:D]
        ps_2m, ps_2r = pY[0][:, D:D + EX], pY[0][0:DR, D + EX:D + 2 * EX]
        ps_2p = pY[1][0:EX, 0:D]
        ps_rank = pX[0][:, 0:NT * EX].rearrange("p (i e) -> p i e", e=EX)
        ps_tot = pX[1][:, 0:NT * EX].rearrange("p (i e) -> p i e", e=EX)
        ps_inv = pY[0][:, 0:ST]

        ids_in = sem("ids_in")
        gathered = [sem(f"gathered{b}") for b in range(B)]
        proj_in, qkv_in, gate_in, tail_in, b2_in, b2p_in = (sem(n) for n in (
            "proj_in", "qkv_in", "gate_in", "tail_in", "b2_in", "b2p_in"))
        consts = sem("consts")
        dve_done = sem("dve_done")
        masks = sem("masks")
        setup_mm, setup_ev = sem("setup_mm"), sem("setup_ev")
        low_mm, low_ev = sem("low_mm"), sem("low_ev")
        h_mm, h_ev, h_norm = sem("h_mm"), sem("h_ev"), sem("h_norm")
        var1, sd1, var2, sd2 = (sem(n) for n in ("var1", "sd1", "var2", "sd2"))
        xT_mm, xT_ev = sem("xT_mm"), sem("xT_ev")
        gram_mm, gram_ev = sem("gram_mm"), sem("gram_ev")
        gv_mm, gv_ev = sem("gv_mm"), sem("gv_ev")
        bb_mm, bb_ev = sem("bb_mm"), sem("bb_ev")
        att_mm, h2_done, x2_done = sem("att_mm"), sem("h2_done"), sem("x2_done")
        x2_out = sem("x2_out")
        x2T_mm, x2T_ev = sem("x2T_mm"), sem("x2T_ev")
        logits = sem("logits")
        lg_ready, lg_exp = sem("lg_ready"), sem("lg_exp")
        picked, counted = sem("picked"), sem("counted")
        hot, inv_mm, routed = sem("hot"), sem("inv_mm"), sem("routed")
        resid = sem("resid")
        token_copied, dest_copied, pool_passed = sem("token_copied"), sem("dest_copied"), sem("pool_passed")
        tok_in = [sem(f"tok_in{u}") for u in range(SLOTS)]
        w_in = [sem(f"w_in{u}") for u in range(SLOTS)]
        sent = [sem(f"sent{u}") for u in range(SLOTS)]
        xs_mm, xs_ev, up_mm, gelu_done, down_mm, y_ev = (sem(n) for n in (
            "xs_mm", "xs_ev", "up_mm", "gelu_done", "down_mm", "y_ev"))
        moe_done = sem("moe_done")
        ys_in = [sem(f"ys_in{b}") for b in range(B)]
        y1w, mix_done, mixT_mm, mixT_ev, proj_mm, fin_done, fin_out = (sem(n) for n in (
            "y1w", "mix_done", "mixT_mm", "mixT_ev", "proj_mm", "fin_done", "fin_out"))
        var3, sd3 = sem("var3"), sem("sd3")

        W1_e = W1.rearrange("g e d h -> (g e) d h")
        b1_e = b1.rearrange("g e h -> (g e) h")
        W2_e = W2.rearrange("g e (p j) d -> (g e) p (j d)", j=HC)
        x_store = x_rows.rearrange("(p i) d -> p i d", i=NT)
        y_load = y_rows[0:K * TOKENS, :].rearrange("(k p i) d -> k p i d", k=K, i=NT)
        out_b = out.rearrange("b (p c) d -> b p c d", c=CB)

        STEPS = B + 2

        def stage(s, off):
            return 0 <= s - off < B

        block = ctx.enter_context(nc.Block())

        @block.sync
        def _(sp):
            with nc.allow_non_contiguous_dma(reason="small weights and ids"):
                sp.dma_start(ids[:, :].rearrange("p (b c) -> p b c", c=CB),
                             x.rearrange("b (p c) -> p b c", c=CB)).then_inc(ids_in, 16)
                for c in range(2):
                    sp.dma_start(proj_m[:, c, :], proj[0:P, :]).then_inc(proj_in, 16)
                    sp.dma_start(proj_r[:, c, :], proj[P:D, :]).then_inc(proj_in, 16)
                for n, (w, b) in enumerate(((Wq, bq), (Wk, bk), (Wv, bv))):
                    col = b.rearrange("(d a) -> d a", a=1)
                    sp.dma_start(qkv_m[:, n, 0:D], w[0:P, :]).then_inc(qkv_in, 16)
                    sp.dma_start(qkv_r[:, n, 0:D], w[P:D, :]).then_inc(qkv_in, 16)
                    sp.dma_start(qkv_m[:, n, D:D1], col[0:P, :]).then_inc(qkv_in, 16)
                    sp.dma_start(qkv_r[:, n, D:D1], col[P:D, :]).then_inc(qkv_in, 16)
                we = We.rearrange("g d e -> d g e")
                sp.dma_start(gate_m[:, 0, :], Wg[0:P, :]).then_inc(gate_in, 16)
                sp.dma_start(gate_r[:, 0, :], Wg[P:D, :]).then_inc(gate_in, 16)
                sp.dma_start(gate_m[:, 1:C, :], we[0:P]).then_inc(gate_in, 16)
                sp.dma_start(gate_r[:, 1:C, :], we[P:D]).then_inc(gate_in, 16)
                sp.dma_start(gate_b[:, 0, :], bg.partition_broadcast(P)).then_inc(gate_in, 16)
                sp.dma_start(gate_b[:, 1:C, :], be.partition_broadcast(P)).then_inc(gate_in, 16)
                sp.dma_start(b2_s[:, :], b2.rearrange("g e d -> (g e) d")).then_inc(b2_in, 16)
                sp.dma_start(Wp_m[:, :], Wp[0:P, :]).then_inc(b2_in, 16)
                sp.dma_start(Wp_r[0:DR, :], Wp[P:D, :]).then_inc(b2_in, 16)
                sp.dma_start(Wp_r[DR + EX:DR + EX + 1, :], bp.rearrange("(a d) -> a d", a=1)).then_inc(tail_in, 16)
                sp.dma_start(gam[:, :], gamma.partition_broadcast(P)).then_inc(tail_in, 16)
                sp.dma_start(bet[:, :], beta.partition_broadcast(P)).then_inc(tail_in, 16)
            sp.wait_ge(setup_ev, 4)
            sp.dma_start(Wp_r[DR:DR + EX, :], b2p[:, :]).then_inc(b2p_in, 16)
            for b in range(B):
                sp.wait_ge(x2_done, b + 1)
                sp.dma_start(x_store[:, CB * b:CB * b + CB, :], x2[:, CB * b:CB * b + CB, :]).then_inc(x2_out, 16)

            sp.wait_ge(routed, 1)

            def load(t, u):
                e = sp.value_load(expert[0:1, bass.ds(t, 1)], min_val=0, max_val=EX - 1)
                sp.dma_start(W1_m[u][:, :], W1_e[bass.ds(e, 1), 0:P, :].rearrange("a d h -> (a d) h")).then_inc(w_in[u], 16)
                sp.dma_start(W1_r[u][0:DR, :], W1_e[bass.ds(e, 1), P:D, :].rearrange("a d h -> (a d) h")).then_inc(w_in[u], 16)
                sp.dma_start(W1_r[u][DR:DR + 1, :], b1_e[bass.ds(e, 1), :]).then_inc(w_in[u], 16)
                sp.dma_start(W2_s[u][:, :, :].rearrange("p j d -> p (j d)"), W2_e[bass.ds(e, 1)].rearrange("a p n -> (a p) n")).then_inc(w_in[u], 16)

            for t in range(SLOTS - 1):
                load(t, t)

            def body(t, u):
                at_least(sp, down_mm, t)
                load(t + SLOTS - 1, (u + SLOTS - 1) % SLOTS)

            for u in range(SLOTS):
                body(u, u)
            with sp.Fori(1, ROUNDS) as i:
                for u in range(SLOTS):
                    body(i * SLOTS + u, u)

            for u in range(SLOTS):
                sp.wait_ge(w_in[u], 64 * (ROUNDS + (u < SLOTS - 1)))
            sp.wait_ge(moe_done, 1)
            for b in range(B):
                for k in range(K):
                    sp.dma_start(ys[:, k, CB * b:CB * b + CB, :], y_load[k, :, CB * b:CB * b + CB, :]).then_inc(ys_in[b], 16)
            for b in range(B):
                sp.wait_ge(fin_done, b + 1)
                sp.dma_start(out_b[b], fin[:, CB * b:CB * b + CB, :]).then_inc(fin_out, 16)
            sp.wait_ge(fin_out, 16 * B)

        @block.gpsimd
        def _(pool):
            iota = dict(allow_small_or_imprecise_dtypes=True)
            pool.iota(diff[:, :], [[1, P]], base=0, channel_multiplier=-1, **iota).then_inc(consts, 1)
            pool.wait_ge(ids_in, 16)
            for i in range(NT):
                pool.indirect_dma_start(emb[:, i, :], None, table, bass.IndirectOffsetOnAxis(
                    ap=ids[:, i:i + 1].bitcast(U32), axis=0)).then_inc(gathered[i // CB], 16)
            pool.iota(lane[:, :], [[1, P]], base=0, channel_multiplier=0, **iota).then_inc(consts, 1)
            pool.iota(rank4[:, :], [[-1, G]], base=G, channel_multiplier=0, **iota).then_inc(consts, 1)
            pool.iota(step128[:, :], [[P, NT]], base=0, channel_multiplier=0, **iota).then_inc(consts, 1)
            pool.iota(tile_no[:, :], [[1, STP]], base=0, channel_multiplier=0, **iota).then_inc(consts, 1)
            pool.iota(row_id[:, 0, :], [[1, NT]], base=1, channel_multiplier=NT, **iota).then_inc(consts, 1)
            pool.iota(row_id[:, 1, :], [[-1, NT]], base=-1, channel_multiplier=-NT, **iota).then_inc(consts, 1)
            pool.iota(dump[:, :, :], [[0, STP // SLOTS], [P, SLOTS]], base=K * TOKENS, channel_multiplier=1, **iota).then_inc(consts, 1)
            pool.wait_ge(tail_in, 48)
            pool.wait_ge(x2_done, B)
            pool.tensor_tensor(h2[:, :, :], h2[:, :, :], bet[:, :].unsqueeze(1).to_broadcast([P, NT, D]),
                               ALU.add).then_inc(resid, 1)

            pool.wait_ge(routed, 1)
            pool.wait_ge(x2_out, 16 * B)

            def gather(t, u):
                pool.tensor_copy(token_i[u][:, :], token_of[:, bass.ds(t, 1)]).then_inc(token_copied, 1)
                pool.wait_ge(token_copied, t + 1)
                pool.sem_inc(pool_passed, 1)
                pool.indirect_dma_start(xg[u][:, :], None, x_rows, bass.IndirectOffsetOnAxis(
                    ap=token_i[u][:, :].bitcast(U32), axis=0)).then_inc(tok_in[u], 16)

            for t in range(SLOTS - 1):
                gather(t, t)

            def body(t, u, i):
                at_least(pool, xs_mm, t)
                gather(t + SLOTS - 1, (u + SLOTS - 1) % SLOTS)
                at_least(pool, sent[u], 16 * i)
                pool.tensor_copy(dest_i[u][:, :], dest_of[:, bass.ds(t, 1)]).then_inc(dest_copied, 1)
                pool.wait_ge(dest_copied, t + 1)
                pool.wait_ge(y_ev, t + 1)
                pool.sem_inc(pool_passed, 1)
                pool.indirect_dma_start(y_rows, bass.IndirectOffsetOnAxis(
                    ap=dest_i[u][:, :].bitcast(U32), axis=0), yo[u][:, :], None).then_inc(sent[u], 16)

            for u in range(SLOTS):
                body(u, u, 0)
            with pool.Fori(1, ROUNDS) as i:
                for u in range(SLOTS):
                    body(i * SLOTS + u, u, i)
            for u in range(SLOTS):
                pool.wait_ge(sent[u], 16 * ROUNDS)
                pool.wait_ge(tok_in[u], 16 * (ROUNDS + (u < SLOTS - 1)))
            pool.sem_inc(moe_done, 1)

        @block.scalar
        def _(act):
            def copy(dst, src, s=None):
                ins = nc.scalar.activation(dst, src, ACT.Copy)
                if s is not None:
                    ins.then_inc(s, 1)

            act.wait_ge(setup_mm, 1)
            copy(projT[:, :], ps_pr, setup_ev)
            act.wait_ge(setup_mm, 2)
            nc.scalar.activation(AT_m[:, :], ps_am, ACT.Copy, scale=float(D) ** -0.5)
            nc.scalar.activation(AT_r[:, :], ps_ar, ACT.Copy, scale=float(D) ** -0.5)
            copy(WvT_m[:, :], ps_wm)
            copy(WvT_r[:, :], ps_wr, setup_ev)
            act.wait_ge(setup_mm, 3)
            copy(b2T_m[:, :], ps_2m)
            copy(b2T_r[:, :], ps_2r, setup_ev)
            act.wait_ge(setup_mm, 4)
            copy(b2p[:, :], ps_2p, setup_ev)

            for s in range(STEPS):
                if stage(s, 0):
                    b = s
                    act.wait_ge(low_mm, b + 1)
                    at_least(act, h_mm, b - 1)
                    copy(lowT[:, b % 2, :], ps_low, low_ev)
                if stage(s, 1):
                    b = s - 1
                    act.wait_ge(gv_mm, b + 1)
                    at_least(act, bb_mm, b - 1)
                    copy(gv_m[:, b % 2, :], ps_vm)
                    copy(gv_r[:, b % 2, :], ps_vr, gv_ev)
                if stage(s, 0):
                    b = s
                    act.wait_ge(h_mm, b + 1)
                    copy(h[:, CB * b, :], ps_h[0])
                    copy(h[:, CB * b + 1, :], ps_h[1], h_ev)
                    act.wait_ge(var1, b + 1)
                    nc.scalar.activation(sd[:, 0, :], ve[:, 0, :], ACT.Sqrt).then_inc(sd1, 1)
                if stage(s, 2):
                    b = s - 2
                    act.wait_ge(x2T_mm, b + 1)
                    at_least(act, logits, b - 1)
                    copy(x2T_m[:, b % 2, :], ps_x2m)
                    copy(x2T_r[:, b % 2, :], ps_x2r, x2T_ev)
                if stage(s, 1):
                    b = s - 1
                    act.wait_ge(bb_mm, b + 1)
                    at_least(act, att_mm, b - 1)
                    copy(bb_m[:, b % 2, :], ps_bm)
                    copy(bb_r[:, b % 2, :], ps_br, bb_ev)
                if stage(s, 0):
                    b = s
                    act.wait_ge(gram_mm, b + 1)
                    at_least(act, gv_mm, b - 1)
                    copy(gram_m[:, b % 2, :], ps_gm)
                    copy(gram_r[:, b % 2, :], ps_gr, gram_ev)
                    act.wait_ge(xT_mm, b + 1)
                    at_least(act, att_mm, b - 1)
                    copy(xT_m[:, b % 2, :], ps_xm)
                    copy(xT_r[:, b % 2, :], ps_xr, xT_ev)
                if stage(s, 1):
                    b = s - 1
                    act.wait_ge(var2, b + 1)
                    nc.scalar.activation(sd[:, 1, :], ve[:, 1, :], ACT.Sqrt).then_inc(sd2, 1)

            act.wait_ge(lg_ready, 1)
            nc.scalar.activation(lg[:, :, :], lx[:, :, :], ACT.Exp).then_inc(lg_exp, 1)

            def body(t, u):
                v = u % 2
                act.wait_ge(up_mm, t + 1)
                at_least(act, down_mm, t - 1)
                nc.scalar.activation(hT[v][:, :], pA[v][:, 0:H], ACT.Gelu).then_inc(gelu_done, 1)

            for u in range(SLOTS):
                body(u, u)
            with act.Fori(1, ROUNDS) as i:
                for u in range(SLOTS):
                    body(i * SLOTS + u, u)

            for i in range(NT + 1):
                if i < NT:
                    act.wait_ge(ys_in[i // CB], 32)
                    nc.scalar.activation(ys[:, 0, i, :], ys[:, 0, i, :], ACT.Copy,
                                         scale=wk[:, 0, i:i + 1]).then_inc(y1w, 1)
                if i >= 1:
                    j = i - 1
                    act.wait_ge(mixT_mm, j + 1)
                    at_least(act, proj_mm, j - 1)
                    copy(mixT_m[:, j % 2, :], pX[j % 2][:, 0:P])
                    copy(mixT_r[:, j % 2, :], pX[j % 2][0:DR + EX + 1, P:2 * P], mixT_ev)
                    if j % CB == CB - 1:
                        b = j // CB
                        act.wait_ge(var3, b + 1)
                        nc.scalar.activation(sd[:, 2, :], ve[:, 2, :], ACT.Sqrt).then_inc(sd3, 1)

        @block.vector
        def _(dve):
            made = [0]

            def link(ins):
                made[0] += 1
                ins.then_inc(dve_done, 1)
                dve.wait_ge(dve_done, made[0])

            nc.vector.memset(ones[:, :], 1.0)
            nc.vector.memset(carry[:, :, :], 1.0)
            nc.vector.memset(unit[:, :], 1.0)
            nc.vector.memset(x2[:, :, D:ROW], 1.0)
            nc.vector.memset(mixw[:, :, D + EX:D + EX + 1], 1.0)
            link(nc.vector.memset(xh[:, :, :, D:D1], 1.0))
            nc.vector.memset(carry[:, :, 0:1], 0.0)
            dve.wait_ge(consts, 1)
            nc.vector.tensor_scalar(ident[:, :], diff[:, :], 0.0, None, ALU.is_equal).then_inc(masks, 1)
            nc.vector.tensor_scalar(before[:, :], diff[:, :], 0.0, None, ALU.is_gt).then_inc(masks, 1)

            def rsqrt(n, ready, root, count):
                nc.vector.tensor_scalar(ve[:, n, :], mv[:, n, :, 1], EPS, None, ALU.add).then_inc(ready, 1)
                dve.wait_ge(root, count)
                link(nc.vector.reciprocal(rs[:, n, :], sd[:, n, :]))
                link(nc.vector.tensor_tensor(tn[:, n, :], rs[:, n, :], rs[:, n, :], ALU.mult))
                link(nc.vector.tensor_tensor(tn[:, n, :], tn[:, n, :], ve[:, n, :], ALU.mult))
                link(nc.vector.tensor_scalar(tn[:, n, :], tn[:, n, :], -0.5, 1.5, ALU.mult, ALU.add))
                link(nc.vector.tensor_tensor(rs[:, n, :], rs[:, n, :], tn[:, n, :], ALU.mult))

            for s in range(STEPS):
                if stage(s, 0):
                    b = s
                    dve.wait_ge(h_ev, b + 1)
                    nc.vector.bn_stats(stats[:, 0, 0, :], h[:, CB * b, :])
                    link(nc.vector.bn_stats(stats[:, 0, 1, :], h[:, CB * b + 1, :]))
                    nc.vector.bn_aggr(mv[:, 0, 0, :], stats[:, 0, 0, :])
                    link(nc.vector.bn_aggr(mv[:, 0, 1, :], stats[:, 0, 1, :]))
                    rsqrt(0, var1, sd1, b + 1)
                    at_least(dve, xT_mm, b - 1)
                    for c in range(CB):
                        ins = nc.vector.tensor_scalar(xh[:, b % 2, c, 0:D], h[:, CB * b + c, :], mv[:, 0, c, 0:1],
                                                      rs[:, 0, c:c + 1], ALU.subtract, ALU.mult)
                    ins.then_inc(h_norm, 1)
                if stage(s, 1):
                    b = s - 1
                    tiles = slice(CB * b, CB * b + CB)
                    dve.wait_ge(att_mm, b + 1)
                    nc.vector.tensor_tensor(h2[:, tiles, :], ps_o, h[:, tiles, :], ALU.add).then_inc(h2_done, 1)
                    dve.wait_ge(h2_done, b + 1)
                    for c in range(CB):
                        ins = nc.vector.bn_stats(stats[:, 1, c, :], h2[:, CB * b + c, :])
                    link(ins)
                    for c in range(CB):
                        ins = nc.vector.bn_aggr(mv[:, 1, c, :], stats[:, 1, c, :])
                    link(ins)
                    rsqrt(1, var2, sd2, b + 1)
                    for c in range(CB):
                        ins = nc.vector.tensor_scalar(x2[:, CB * b + c, 0:D], h2[:, CB * b + c, :], mv[:, 1, c, 0:1],
                                                      rs[:, 1, c:c + 1], ALU.subtract, ALU.mult)
                    ins.then_inc(x2_done, 1)

            V = nc.vector
            dve.wait_ge(logits, B)
            dve.wait_ge(gate_in, 96)
            dve.wait_ge(consts, 8)
            N = NT * C
            lg_v = lg[:, :, :].rearrange("p (i c) e -> p i (c e)", c=C)
            link(V.tensor_tensor(lg_v, ps_lg.rearrange("p (i n) -> p i n", i=NT),
                                 gate_b[:, :, :].rearrange("p c e -> p (c e)").unsqueeze(1).to_broadcast([P, NT, 4 * C]),
                                 ALU.add))
            link(V.tensor_reduce(r4[:, :], lg[:, :, :], AX.X, ALU.max))
            V.tensor_tensor(lx[:, :, :], lg[:, :, :], r4[:, :].unsqueeze(2).to_broadcast([P, N, 4]),
                            ALU.subtract).then_inc(lg_ready, 1)
            dve.wait_ge(lg_exp, 1)
            link(V.tensor_reduce(r4[:, :], lg[:, :, :], AX.X, ALU.add))
            link(V.reciprocal(r4[:, :], r4[:, :]))
            pr_v = pr[:, :, :, :].rearrange("p i c e -> p (i c) e")
            link(V.tensor_tensor(pr_v, lg[:, :, :], r4[:, :].unsqueeze(2).to_broadcast([P, N, 4]), ALU.mult))

            def top(chosen, best, prob, n, keys, kbest):
                link(V.tensor_reduce(best, prob, AX.X, ALU.max))
                link(V.tensor_tensor(chosen, prob, best.unsqueeze(2).to_broadcast([P, n, 4]), ALU.is_equal))
                link(V.tensor_tensor(keys, chosen, rank4[:, :].unsqueeze(1).to_broadcast([P, n, 4]), ALU.mult))
                link(V.tensor_reduce(kbest, keys, AX.X, ALU.max))
                link(V.tensor_tensor(chosen, keys, kbest.unsqueeze(2).to_broadcast([P, n, 4]), ALU.is_equal))

            top(first[:, :, :, :].rearrange("p i c e -> p (i c) e"), pmax[:, :, :].rearrange("p i c -> p (i c)"),
                pr_v, N, key[:, :, :], kmax[:, :])
            link(V.scalar_tensor_tensor(out=pg2[:, :, :], in0=first[:, :, 0, :], scalar=-4.0, in1=pr[:, :, 0, :],
                                        op0=ALU.mult, op1=ALU.add))
            top(second[:, :, :], gmax2[:, :], pg2[:, :, :], NT, key[:, 0:NT, :], kmax[:, 0:NT])
            groups = (first[:, :, 0, :], second[:, :, :])
            gws = (pmax[:, :, 0], gmax2[:, :])
            for k in range(K):
                ins = V.tensor_tensor(sel[:, k, :, :].rearrange("p i (g e) -> p i g e", g=G),
                                      groups[k].unsqueeze(3).to_broadcast([P, NT, G, E]),
                                      first[:, :, 1:C, :], ALU.mult)
            link(ins)
            V.tensor_tensor(both[:, :, :], sel[:, 0, :, :], sel[:, 1, :, :], ALU.add).then_inc(picked, 1)
            for k in range(K):
                link(V.tensor_tensor(wg_[:, :, :], groups[k], pmax[:, :, 1:C], ALU.mult))
                link(V.tensor_reduce(wk[:, k, :], wg_[:, :, :], AX.X, ALU.add))
                link(V.tensor_tensor(wk[:, k, :], wk[:, k, :], gws[k], ALU.mult))
            dve.wait_ge(counted, 1)
            link(V.tensor_copy(total[:, :, :], ps_tot.rearrange("p i e -> p e i")))
            link(V.tensor_tensor_scan(upto[:, :, :].rearrange("p e i -> p (e i)"),
                                      carry[:, :, :].rearrange("p e i -> p (e i)"),
                                      total[:, :, :].rearrange("p e i -> p (e i)"), 0.0, ALU.mult, ALU.add))
            link(V.tensor_tensor(more[:, :, :], upto[:, :, NT - 1:NT].to_broadcast([P, EX, NT]),
                                 step128[:, :].unsqueeze(1).to_broadcast([P, EX, NT]), ALU.is_gt))
            link(V.tensor_reduce(tiles_e[:, :], more[:, :, :], AX.X, ALU.add))
            link(V.tensor_tensor_scan(end_e[:, :], unit[:, :], tiles_e[:, :], 0.0, ALU.mult, ALU.add))
            link(V.tensor_tensor(base_e[:, :], end_e[:, :], tiles_e[:, :], ALU.subtract))
            link(V.tensor_scalar(base_e[:, :], base_e[:, :], float(P), None, ALU.mult))
            link(V.tensor_tensor(upto[:, :, :], upto[:, :, :], total[:, :, :], ALU.subtract))
            link(V.tensor_tensor(upto[:, :, :], upto[:, :, :], base_e[:, :].unsqueeze(2).to_broadcast([P, EX, NT]), ALU.add))
            link(V.tensor_tensor(place[:, :, :], ps_rank, upto[:, :, :].rearrange("p e i -> p i e"), ALU.add))
            link(V.tensor_tensor(placed[:, :, :, :], sel[:, :, :, :],
                                 place[:, :, :].unsqueeze(1).to_broadcast([P, K, NT, EX]), ALU.mult))
            link(V.tensor_reduce(slot_f[:, :], placed[:, :, :, :].rearrange("p k i e -> p (k i) e"), AX.X, ALU.add))
            link(V.tensor_copy(slot_i[:, :], slot_f[:, :]))
            V.tensor_scalar(slot_t[:, 0, :], slot_i[:, :], 7, None, ALU.arith_shift_right)
            link(V.tensor_scalar(slot_t[:, 1, :], slot_i[:, :], P - 1, None, ALU.bitwise_and))
            link(V.tensor_copy(slot_p[:, :, :], slot_t[:, :, :]))
            rows = row_id[:, :, :].rearrange("p k i -> p (k i)")
            for m in range(K * NT):
                V.tensor_scalar(hot_lane[:, m, :], lane[:, :], slot_p[:, 1, m:m + 1], None, ALU.is_equal)
                V.tensor_scalar(hot_tile[:, m, :], lane[:, 0:ST], slot_p[:, 0, m:m + 1], rows[:, m:m + 1],
                                ALU.is_equal, ALU.mult).then_inc(hot, 1)
            link(V.tensor_tensor(past[:, :, :], tile_no[0:1, :].unsqueeze(2).to_broadcast([1, STP, EX]),
                                 end_e[0:1, :].unsqueeze(1).to_broadcast([1, STP, EX]), ALU.is_ge))
            link(V.tensor_reduce(expert_f[:, :], past[:, :, :], AX.X, ALU.add))
            link(V.tensor_scalar(expert[:, :], expert_f[:, :], float(EX - 1), None, ALU.min))
            link(V.memset(inv[:, :, :], 0.0))
            dve.wait_ge(inv_mm, 1)
            link(V.tensor_copy(inv[:, 0, 0:ST], ps_inv))
            V.tensor_scalar(inv[:, 1, :], inv[:, 0, :], 0.0, float(TOKENS), ALU.is_lt, ALU.mult)
            link(V.tensor_scalar(inv[:, 2, :], inv[:, 0, :], -1.0, None, ALU.mult))
            link(V.tensor_tensor(inv[:, 2, :], inv[:, 2, :], inv[:, 0, :], ALU.max))
            V.tensor_scalar(inv[:, 3, :], inv[:, 2, :], 0.5, None, ALU.is_gt)
            link(V.tensor_scalar(inv[:, 2, :], inv[:, 2, :], -1.0, 0.0, ALU.add, ALU.max))
            V.tensor_copy(token_of[:, :], inv[:, 2, :])
            link(V.tensor_tensor(inv[:, 4, :], inv[:, 2, :], inv[:, 1, :], ALU.add))
            spare = dump[:, :, :].rearrange("p a b -> p (a b)")
            link(V.tensor_tensor(inv[:, 5, :], inv[:, 4, :], spare, ALU.subtract))
            link(V.tensor_tensor(inv[:, 5, :], inv[:, 5, :], inv[:, 3, :], ALU.mult))
            V.tensor_tensor(dest_of[:, :], inv[:, 5, :], spare, ALU.add).then_inc(routed, 1)
            for k in range(K):
                V.tensor_tensor(placed[:, k, :, :], sel[:, k, :, :],
                                wk[:, k, :].unsqueeze(2).to_broadcast([P, NT, EX]), ALU.mult)
            link(V.tensor_copy(wsel[:, :, :], sel[:, 0, :, :]))
            link(V.tensor_tensor(mixw[:, :, D:D + EX], placed[:, 0, :, :], placed[:, 1, :, :], ALU.add))

            def turned(t, v):
                dve.wait_ge(xs_mm, t + 1)
                at_least(dve, up_mm, t - 1)
                V.tensor_copy(xs_m[v][:, :], pX[v][:, 0:P])
                V.tensor_copy(xs_r[v][:, :], pX[v][0:DR + 1, P:2 * P]).then_inc(xs_ev, 1)

            turned(0, 0)
            turned(1, 1)

            def body(t, u, i):
                v = u % 2
                turned(t + 2, v)
                dve.wait_ge(down_mm, t + 1)
                at_least(dve, sent[u], 16 * i)
                V.tensor_copy(yo[u][:, :], pY[v][:, 0:D]).then_inc(y_ev, 1)

            for u in range(SLOTS):
                body(u, u, 0)
            with dve.Fori(1, ROUNDS) as i:
                for u in range(SLOTS):
                    body(i * SLOTS + u, u, i)

            dve.wait_ge(resid, 1)
            for i in range(NT + 2):
                if i < NT:
                    dve.wait_ge(y1w, i + 1)
                    V.scalar_tensor_tensor(out=mixw[:, i, 0:D], in0=ys[:, 1, i, :], scalar=wk[:, 1, i:i + 1],
                                           in1=ys[:, 0, i, :], op0=ALU.mult, op1=ALU.add).then_inc(mix_done, 1)
                if i >= CB and i % CB == 0:
                    b = i // CB - 1
                    dve.wait_ge(proj_mm, CB * b + CB)
                    for c in range(CB):
                        ins = V.bn_stats(stats[:, 0, c, :], pY[c][:, 0:D])
                    link(ins)
                    for c in range(CB):
                        ins = V.bn_aggr(mv[:, 2, c, :], stats[:, 0, c, :])
                    link(ins)
                    rsqrt(2, var3, sd3, b + 1)
                    for c in range(CB):
                        j = CB * b + c
                        ins = V.scalar_tensor_tensor(out=fin[:, j, :], in0=pY[c][:, 0:D], scalar=mv[:, 2, c, 0:1],
                                                     in1=gam[:, :], op0=ALU.subtract, op1=ALU.mult)
                    link(ins)
                    for c in range(CB):
                        j = CB * b + c
                        ins = V.scalar_tensor_tensor(out=fin[:, j, :], in0=fin[:, j, :], scalar=rs[:, 2, c:c + 1],
                                                     in1=h2[:, j, :], op0=ALU.mult, op1=ALU.add)
                    ins.then_inc(fin_done, 1)

        @block.tensor
        def _(pe):
            def two(out_ap, m_l, m_r, r_l, r_r):
                pe.matmul(out_ap, m_l, r_l, start=True, stop=False)
                return pe.matmul(out_ap, m_r, r_r, start=False, stop=True)

            pe.wait_ge(masks, 2)
            pe.wait_ge(proj_in, 64)
            pe.transpose(ps_pr[:, 0:P], proj_m[:, :, :].rearrange("p c r -> p (c r)"), ident[:, :])
            pe.transpose(ps_pr[:, P:D], proj_r[:, :, :].rearrange("p c r -> p (c r)"), ident[0:DR, 0:DR]).then_inc(setup_mm, 1)
            pe.wait_ge(qkv_in, 16 * 12)
            two(ps_am, qkv_m[:, 1, 0:P], qkv_r[:, 1, 0:P], qkv_m[:, 0, :], qkv_r[:, 0, :])
            two(ps_ar, qkv_m[:, 1, P:D1], qkv_r[:, 1, P:D1], qkv_m[:, 0, :], qkv_r[:, 0, :])
            pe.transpose(ps_wm[:, 0:P], qkv_m[:, 2, 0:P], ident[:, :])
            pe.transpose(ps_wm[:, P:D], qkv_r[:, 2, 0:P], ident[0:DR, 0:DR])
            pe.transpose(ps_wr[:, 0:P], qkv_m[:, 2, P:D1], ident[:, :])
            pe.transpose(ps_wr[:, P:D], qkv_r[:, 2, P:D1], ident[0:DR, 0:DR]).then_inc(setup_mm, 1)
            pe.wait_ge(b2_in, 48)
            pe.wait_ge(setup_ev, 1)
            pe.transpose(ps_2m, b2_s[:, 0:P], ident[0:EX, 0:EX])
            pe.transpose(ps_2r, b2_s[:, P:D], ident[0:EX, 0:EX]).then_inc(setup_mm, 1)
            pe.wait_ge(setup_ev, 3)
            two(ps_2p, b2T_m[:, :], b2T_r[:, :], Wp_m[:, :], Wp_r[0:DR, :]).then_inc(setup_mm, 1)
            pe.wait_ge(setup_ev, 4)

            for s in range(STEPS):
                if stage(s, 0):
                    b = s
                    pe.wait_ge(gathered[b], 16 * CB)
                    at_least(pe, low_ev, b)
                    pe.transpose(ps_low, emb[:, CB * b:CB * b + CB, :].rearrange("p c r -> p (c r)"),
                                 ident[:, :]).then_inc(low_mm, 1)
                if stage(s, 1):
                    b = s - 1
                    q = b % 2
                    pe.wait_ge(gram_ev, b + 1)
                    at_least(pe, gv_ev, b)
                    two(ps_vm, gram_m[:, q, 0:P], gram_r[:, q, 0:P], WvT_m[:, :], WvT_r[:, :])
                    two(ps_vr, gram_m[:, q, P:D1], gram_r[:, q, P:D1], WvT_m[:, :], WvT_r[:, :]).then_inc(gv_mm, 1)
                if stage(s, 0):
                    b = s
                    pe.wait_ge(low_ev, b + 1)
                    at_least(pe, h_ev, b)
                    for c in range(CB):
                        mm = pe.matmul(ps_h[c], lowT[c * RANK:(c + 1) * RANK, b % 2, :],
                                       projT[c * RANK:(c + 1) * RANK, :], start=True, stop=True)
                    mm.then_inc(h_mm, 1)
                if stage(s, 2):
                    b = s - 2
                    pe.wait_ge(x2_done, b + 1)
                    pe.wait_ge(xT_ev, min(b + 2, B))
                    for c in range(CB):
                        pe.transpose(ps_x2m[:, c * P:(c + 1) * P], x2[:, CB * b + c, 0:P], ident[:, :])
                        mm = pe.transpose(ps_x2r[:, c * P:(c + 1) * P], x2[:, CB * b + c, P:D], ident[:, :])
                    mm.then_inc(x2T_mm, 1)
                if stage(s, 1):
                    b = s - 1
                    q = b % 2
                    pe.wait_ge(gv_ev, b + 1)
                    at_least(pe, bb_ev, b)
                    two(ps_bm, AT_m[:, 0:P], AT_r[:, 0:P], gv_m[:, q, :], gv_r[:, q, :])
                    two(ps_br, AT_m[:, P:D1], AT_r[:, P:D1], gv_m[:, q, :], gv_r[:, q, :]).then_inc(bb_mm, 1)
                if stage(s, 2):
                    b = s - 2
                    if b == 0:
                        pe.wait_ge(gate_in, 96)
                    pe.wait_ge(x2T_ev, b + 1)
                    for c in range(CB):
                        i = CB * b + c
                        mm = two(ps_lg[:, i * 4 * C:(i + 1) * 4 * C], x2T_m[:, b % 2, c * P:(c + 1) * P],
                                 x2T_r[:, b % 2, c * P:(c + 1) * P],
                                 gate_m[:, :, :].rearrange("p c e -> p (c e)"), gate_r[:, :, :].rearrange("p c e -> p (c e)"))
                    mm.then_inc(logits, 1)
                if stage(s, 1):
                    b = s - 1
                    q = b % 2
                    pe.wait_ge(bb_ev, b + 1)
                    pe.wait_ge(xT_ev, b + 1)
                    at_least(pe, h2_done, b)
                    for c in range(CB):
                        mm = two(ps_o[:, c, :], xT_m[:, q, c * P:(c + 1) * P], xT_r[:, q, c * P:(c + 1) * P],
                                 bb_m[:, q, :], bb_r[:, q, :])
                    mm.then_inc(att_mm, 1)
                if stage(s, 0):
                    b = s
                    q = b % 2
                    pe.wait_ge(h_norm, b + 1)
                    at_least(pe, gram_ev, b)
                    for rows, lo, hi in ((ps_gm, 0, P), (ps_gr, P, D1)):
                        for c in range(CB):
                            mm = pe.matmul(rows, xh[:, q, c, lo:hi], xh[:, q, c, :], start=(c == 0), stop=(c == CB - 1))
                    mm.then_inc(gram_mm, 1)
                    at_least(pe, x2T_ev, b - 1)
                    for c in range(CB):
                        pe.transpose(ps_xm[:, c * P:(c + 1) * P], xh[:, q, c, 0:P], ident[:, :])
                        mm = pe.transpose(ps_xr[:, c * P:(c + 1) * P], xh[:, q, c, P:D1], ident[:, :])
                    mm.then_inc(xT_mm, 1)

            pe.wait_ge(picked, 1)
            chosen = both[:, :, :].rearrange("p i e -> p (i e)")
            pe.matmul(ps_rank.rearrange("p i e -> p (i e)"), before[:, :], chosen, start=True, stop=True)
            pe.matmul(ps_tot.rearrange("p i e -> p (i e)"), ones[:, :], chosen, start=True, stop=True).then_inc(counted, 1)
            for m in range(K * NT):
                pe.wait_ge(hot, m + 1)
                mm = pe.matmul(ps_inv, hot_lane[:, m, :], hot_tile[:, m, :], start=(m == 0), stop=(m == K * NT - 1))
            mm.then_inc(inv_mm, 1)

            def turn(t, u, loads):
                v = u % 2
                pe.wait_ge(tok_in[u], loads)
                at_least(pe, xs_ev, t - 1)
                pe.transpose(pX[v][:, 0:P], xg[u][:, 0:P], ident[:, :])
                pe.transpose(pX[v][0:DR + 1, P:2 * P], xg[u][:, P:D1], ident[:, :]).then_inc(xs_mm, 1)

            def up(t, u, loads):
                v = u % 2
                pe.wait_ge(xs_ev, t + 1)
                pe.wait_ge(w_in[u], loads)
                at_least(pe, gelu_done, t - 1)
                for j in range(HC):
                    mm = two(pA[v][:, j * P:(j + 1) * P], W1_m[u][:, j::HC], W1_r[u][:, j::HC], xs_m[v][:, :], xs_r[v][:, :])
                mm.then_inc(up_mm, 1)

            def down(t, u):
                v = u % 2
                pe.wait_ge(gelu_done, t + 1)
                at_least(pe, y_ev, t - 1)
                for j in range(HC):
                    mm = pe.matmul(pY[v][:, 0:D], hT[v][:, j * P:(j + 1) * P], W2_s[u][:, j, :],
                                   start=(j == 0), stop=(j == HC - 1))
                mm.then_inc(down_mm, 1)

            turn(0, 0, 16)
            turn(1, 1, 16)
            up(0, 0, 64)

            def body(t, u, i):
                turn(t + 2, (u + 2) % SLOTS, 16 * (i + (2 if u >= SLOTS - 2 else 1)))
                up(t + 1, (u + 1) % SLOTS, 64 * (i + (2 if u == SLOTS - 1 else 1)))
                down(t, u)

            for u in range(SLOTS):
                body(u, u, 0)
            with pe.Fori(1, ROUNDS) as i:
                for u in range(SLOTS):
                    body(i * SLOTS + u, u, i)

            for i in range(NT + 1):
                if i < NT:
                    if i == 0:
                        pe.wait_ge(xs_ev, ST + 2)
                    pe.wait_ge(mix_done, i + 1)
                    at_least(pe, mixT_ev, i - 1)
                    pe.transpose(pX[i % 2][:, 0:P], mixw[:, i, 0:P], ident[:, :])
                    pe.transpose(pX[i % 2][0:DR + EX + 1, P:2 * P], mixw[:, i, P:D + EX + 1], ident[:, :]).then_inc(mixT_mm, 1)
                if i >= 1:
                    j = i - 1
                    if j == 0:
                        pe.wait_ge(b2p_in, 16)
                        pe.wait_ge(tail_in, 48)
                    pe.wait_ge(mixT_ev, j + 1)
                    at_least(pe, fin_done, j // CB)
                    two(pY[j % CB][:, 0:D], mixT_m[:, j % 2, :], mixT_r[:, j % 2, :], Wp_m[:, :], Wp_r[:, :]).then_inc(proj_mm, 1)


_INS = ["x", "L0_tok_embed_table", "L0_tok_proj_up", "L0_attn_Wq", "L0_attn_bq", "L0_attn_Wk", "L0_attn_bk", "L0_attn_Wv",
        "L0_attn_bv", "L0_ffn_Wg", "L0_ffn_bg", "L0_ffn_We", "L0_ffn_be", "L0_ffn_W1", "L0_ffn_b1", "L0_ffn_W2",
        "L0_ffn_b2", "L0_ffn_Wp", "L0_ffn_bp", "L0_ffn_gamma", "L0_ffn_beta"]


def kernel(**inputs):
    import concourse.bacc as _bacc
    from concourse.bass_utils import run_bass_kernel_spmd as _run

    nc = _bacc.Bacc("TRN2", target_bir_lowering=False, num_devices=1)
    arrays, args = {}, []
    for name in _INS:
        a = np.ascontiguousarray(inputs[name])
        arrays[f"in_{name}_dram"] = a
        args.append(nc.dram_tensor(f"in_{name}_dram", a.shape, mybir.dt.from_np(a.dtype), kind="ExternalInput").ap())
    shape = (*inputs["x"].shape, inputs["L0_tok_proj_up"].shape[0])
    out = nc.dram_tensor("out_0_dram", shape, F32, kind="ExternalOutput").ap()
    lm_tower(nc, *args, out)
    r = _run(nc, [arrays], core_ids=[0])
    return r.results[0]["out_0_dram"]
```

```python
from contextlib import ExitStack

import numpy as np

import concourse.bass as bass
from concourse import mybir

F32 = mybir.dt.float32
F16 = mybir.dt.float16
BF16 = mybir.dt.bfloat16
I32 = mybir.dt.int32
U32 = mybir.dt.uint32
ALU = mybir.AluOpType
ACT = mybir.ActivationFunctionType
AX = mybir.AxisListType

P = 128
EPS = 1e-5


def at_least(eng, sem, count):
    if isinstance(count, int) and count <= 0:
        return
    eng.wait_ge(sem, count)


def lm_tower(nc, x, table, proj, Wq, bq, Wk, bk, Wv, bv, Wg, bg, We, be, W1, b1, W2, b2, Wp, bp, gamma, beta, out):
    B, S = x.shape
    VOCAB, RANK = table.shape
    D = proj.shape[0]
    G, E = We.shape[0], We.shape[2]
    H = W1.shape[3]
    NT = B * S // P
    TOKENS = NT * P
    CB = S // P
    DR = D - P
    D1 = D + 1
    EX = G * E
    K = 2
    HC = H // P
    C = 1 + G
    SLOTS = 4
    ROUNDS = -(-(K * TOKENS // P + EX - 1) // SLOTS)
    ST = ROUNDS * SLOTS
    STP = ST + 2 * SLOTS
    OWN = 24
    FULL = K * TOKENS // P // SLOTS
    assert (CB, RANK, K) == (2, 64, 2) and HC * P == H and S == CB * P

    ROW = 200
    x_rows = nc.dram_tensor("x_rows", [TOKENS, ROW], F32).ap()
    y_rows = nc.dram_tensor("y_rows", [K * TOKENS + SLOTS * P, D], F32).ap()

    with ExitStack() as ctx:
        def sb(name, shape, dt=F32):
            return ctx.enter_context(nc.sbuf_tensor(name, shape, dt))

        def sem(name):
            return ctx.enter_context(nc.semaphore(name))

        diff = sb("diff", [P, P])
        ident = sb("ident", [P, P])
        before = sb("before", [P, P], BF16)
        ones = sb("ones", [P, P], BF16)
        lane = sb("lane", [P, P], F16)
        rank4 = sb("rank4", [P, G])
        step128 = sb("step128", [P, NT])
        tile_no = sb("tile_no", [P, STP])
        carry = sb("carry", [P, EX, NT])
        row_id = sb("row_id", [P, K, NT])
        dump = sb("dump", [P, STP // SLOTS, SLOTS])
        ids = sb("ids", [P, NT], I32)
        proj_s = sb("proj_s", [D // 2, 2, 2, RANK])
        projT = sb("projT", [P, D])
        qkv = sb("qkv", [D // 2, 3, 2, D1])
        AT_m = sb("AT_m", [P, D1])
        AT_r = sb("AT_r", [DR + 1, D1])
        WvT_m = sb("WvT_m", [P, D])
        WvT_r = sb("WvT_r", [DR + 1, D])
        gate_m = sb("gate_m", [P, C, 4])
        gate_r = sb("gate_r", [DR, C, 4])
        gate_b = sb("gate_b", [P, C, 4])
        Wp_m = sb("Wp_m", [P, D])
        Wp_r = sb("Wp_r", [DR + EX + 1, D])
        b2_s = sb("b2_s", [EX, D])
        b2T_m = sb("b2T_m", [P, EX])
        b2T_r = sb("b2T_r", [DR, EX])
        b2p = sb("b2p", [EX, D])
        gam = sb("gam", [P, D])
        bet = sb("bet", [P, D])
        emb = sb("emb", [P, NT, RANK])
        lowT = sb("lowT", [P, 2, P])
        h = sb("h", [P, NT, D])
        h2 = sb("h2", [P, NT, D])
        xh = sb("xh", [P, 2, CB, D1])
        xT_m = sb("xT_m", [P, 2, CB * P])
        xT_r = sb("xT_r", [DR + 1, 2, CB * P])
        gram_m = sb("gram_m", [P, 2, D1])
        gram_r = sb("gram_r", [DR + 1, 2, D1])
        gv_m = sb("gv_m", [P, 2, D])
        gv_r = sb("gv_r", [DR + 1, 2, D])
        bb_m = sb("bb_m", [P, 2, D])
        bb_r = sb("bb_r", [DR + 1, 2, D])
        x2 = sb("x2", [P, NT, ROW])
        x2T_m = sb("x2T_m", [P, 2, CB * P])
        x2T_r = sb("x2T_r", [DR, 2, CB * P])
        stats = sb("stats", [P, 2, CB, 6])
        mv = sb("mv", [P, 3, CB, 2])
        ve = sb("ve", [P, 3, CB])
        sd = sb("sd", [P, 3, CB])
        rs = sb("rs", [P, 3, CB])
        tn = sb("tn", [P, 3, CB])
        lg = sb("lg", [P, NT * C, 4])
        lx = sb("lx", [P, NT * C, 4])
        r4 = sb("r4", [P, NT * C])
        pr = sb("pr", [P, NT, C, 4])
        pmax = sb("pmax", [P, NT, C])
        first = sb("first", [P, NT, C, 4])
        key = sb("key", [P, NT * C, 4])
        kmax = sb("kmax", [P, NT * C])
        pg2 = sb("pg2", [P, NT, G])
        second = sb("second", [P, NT, G])
        gmax2 = sb("gmax2", [P, NT])
        sel = sb("sel", [P, K, NT, EX])
        both = sb("both", [P, NT, EX], BF16)
        wg_ = sb("wg_", [P, NT, G])
        wk = sb("wk", [P, K, NT])
        total = sb("total", [P, EX, NT])
        upto = sb("upto", [P, EX, NT])
        more = sb("more", [P, EX, NT])
        tiles_e = sb("tiles_e", [P, EX])
        end_e = sb("end_e", [P, EX])
        unit = sb("unit", [P, EX])
        base_e = sb("base_e", [P, EX])
        past = sb("past", [1, STP, EX])
        expert_f = sb("expert_f", [1, STP])
        expert = sb("expert", [1, STP], I32)
        tiles_used = sb("tiles_used", [1, 1], I32)
        place = sb("place", [P, NT, EX])
        placed = sb("placed", [P, K, NT, EX])
        slot_f = sb("slot_f", [P, K * NT])
        slot_i = sb("slot_i", [P, K * NT], I32)
        slot_t = sb("slot_t", [P, 2, K * NT], I32)
        slot_p = sb("slot_p", [P, 2, K * NT])
        inv = sb("inv", [P, 6, STP])
        token_of = sb("token_of", [P, STP], I32)
        dest_of = sb("dest_of", [P, STP], I32)
        mixw = sb("mixw", [P, NT, D + EX + 1])
        wsel = sb("wsel", [P, NT, EX])
        token_i = [sb(f"token_i{u}", [P, 1], I32) for u in range(SLOTS)]
        dest_i = [sb(f"dest_i{u}", [P, 1], I32) for u in range(SLOTS)]
        xg = [sb(f"xg{u}", [P, ROW]) for u in range(SLOTS)]
        xs_m = [sb(f"xs_m{u}", [P, P]) for u in range(2)]
        xs_r = [sb(f"xs_r{u}", [DR + 1, P]) for u in range(2)]
        W1_m = [sb(f"W1_m{u}", [P, H]) for u in range(SLOTS)]
        W1_r = [sb(f"W1_r{u}", [DR + 1, H]) for u in range(SLOTS)]
        W2_s = [sb(f"W2_s{u}", [P, HC, D]) for u in range(SLOTS)]
        hT = [sb(f"hT{u}", [P, H]) for u in range(2)]
        yo = [sb(f"yo{u}", [P, D]) for u in range(SLOTS)]
        ys = sb("ys", [P, K, NT, D])
        room = ys[:, 0, :, :].rearrange("p i d -> p (i d)").bitcast(F16)
        hot_lane = room[:, 0:K * NT * P].rearrange("p (m l) -> p m l", l=P)
        hot_tile = room[:, K * NT * P:K * NT * (P + ST)].rearrange("p (m t) -> p m t", t=ST)
        mixT_m = sb("mixT_m", [P, 2, P])
        mixT_r = sb("mixT_r", [DR + EX + 1, 2, P])
        nm = sb("nm", [P, CB])
        idle = sb("idle", [P, 1])
        fin = h

        pA = [ctx.enter_context(nc.psum_tensor(f"pA{u}", [P, 1024], F32)) for u in range(2)]
        pX = [ctx.enter_context(nc.psum_tensor(f"pX{u}", [P, 512], F32)) for u in range(2)]
        pY = [ctx.enter_context(nc.psum_tensor(f"pY{u}", [P, 512], F32)) for u in range(2)]
        ps_low = pA[0][:, 0:P]
        ps_lg = pA[0][:, P:P + NT * C * 4]
        ps_h = [pA[0][:, 512:512 + D], pA[1][:, 0:D]]
        ps_xm = pA[1][:, 512:512 + CB * P]
        ps_xr = pA[1][0:DR + 1, 512 + CB * P:1024]
        ps_x2m, ps_x2r = ps_xm, ps_xr[0:DR, :]
        ps_gm, ps_gr = pX[0][:, 0:D1], pX[0][0:DR + 1, D1:2 * D1]
        ps_vm, ps_vr = pX[1][:, 0:D], pX[1][0:DR + 1, D:2 * D]
        ps_bm, ps_br = pY[0][:, 0:D], pY[0][0:DR + 1, D:2 * D]
        ps_o = pY[1][:, 0:CB * D].rearrange("p (c d) -> p c d", c=CB)
        ps_am, ps_ar = pX[0][:, 0:D1], pX[0][0:DR + 1, D1:2 * D1]
        ps_wm, ps_wr = pX[1][:, 0:D], pX[1][0:DR + 1, D:2 * D]
        ps_pr = pY[0][:, 0:D]
        ps_2m, ps_2r = pY[0][:, D:D + EX], pY[0][0:DR, D + EX:D + 2 * EX]
        ps_2p = pY[1][0:EX, 0:D]
        ps_rank = pX[0][:, 0:NT * EX].rearrange("p (i e) -> p i e", e=EX)
        ps_tot = pX[1][:, 0:NT * EX].rearrange("p (i e) -> p i e", e=EX)
        ps_inv = pY[0][:, 0:ST]

        ps_y = [[pY[c][:, 0:D] for c in range(CB)]] + [[pA[u][:, 512 * c:512 * c + D] for c in range(CB)] for u in range(2)]

        ids_in = sem("ids_in")
        gathered = [sem(f"gathered{b}") for b in range(B)]
        proj_in, qkv_in, gate_in, tail_in, b2_in, b2p_in = (sem(n) for n in (
            "proj_in", "qkv_in", "gate_in", "tail_in", "b2_in", "b2p_in"))
        consts, idle_set = sem("consts"), sem("idle_set")
        dve_done = sem("dve_done")
        masks = sem("masks")
        setup_mm, setup_ev = sem("setup_mm"), sem("setup_ev")
        low_mm, low_ev = sem("low_mm"), sem("low_ev")
        h_mm, h_ev, h_norm = sem("h_mm"), sem("h_ev"), sem("h_norm")
        var1, sd1, var2, sd2 = (sem(n) for n in ("var1", "sd1", "var2", "sd2"))
        xT_mm, xT_ev = sem("xT_mm"), sem("xT_ev")
        gram_mm, gram_ev = sem("gram_mm"), sem("gram_ev")
        gv_mm, gv_ev = sem("gv_mm"), sem("gv_ev")
        bb_mm, bb_ev = sem("bb_mm"), sem("bb_ev")
        att_mm, h2_done, x2_done = sem("att_mm"), sem("h2_done"), sem("x2_done")
        x2_out = sem("x2_out")
        x2T_mm, x2T_ev = sem("x2T_mm"), sem("x2T_ev")
        logits = sem("logits")
        lg_ready, lg_exp = sem("lg_ready"), sem("lg_exp")
        picked, counted = sem("picked"), sem("counted")
        hot, hot_t, inv_mm, routed, pool_done, slots_known, ends_known, experts_known, proj_twice = (sem(n) for n in (
            "hot", "hot_t", "inv_mm", "routed", "pool_done", "slots_known", "ends_known", "experts_known", "proj_twice"))
        resid = sem("resid")
        token_copied, dest_copied, pool_passed = sem("token_copied"), sem("dest_copied"), sem("pool_passed")
        tok_in = [sem(f"tok_in{u}") for u in range(SLOTS)]
        w_in = [sem(f"w_in{u}") for u in range(SLOTS)]
        sent = [sem(f"sent{u}") for u in range(SLOTS)]
        xs_mm, xs_ev, up_mm, gelu_done, down_mm, y_ev = (sem(n) for n in (
            "xs_mm", "xs_ev", "up_mm", "gelu_done", "down_mm", "y_ev"))
        moe_done = sem("moe_done")
        ys_in = [sem(f"ys_in{b}") for b in range(B)]
        y1w, mix_done, mixT_mm, mixT_ev, proj_mm, fin_done, fin_out = (sem(n) for n in (
            "y1w", "mix_done", "mixT_mm", "mixT_ev", "proj_mm", "fin_done", "fin_out"))
        var3, sd3, root_step, norm3, z_done, gam_done = (sem(n) for n in (
            "var3", "sd3", "root_step", "norm3", "z_done", "gam_done"))

        W1_e = W1.rearrange("g e d h -> (g e) d h")
        b1_e = b1.rearrange("g e h -> (g e) h")
        W2_e = W2.rearrange("g e (p j) d -> (g e) p (j d)", j=HC)
        x_store = x_rows.rearrange("(p i) d -> p i d", i=NT)
        y_load = y_rows[0:K * TOKENS, :].rearrange("(k p i) d -> k p i d", k=K, i=NT)
        out_b = out.rearrange("b (p c) d -> b p c d", c=CB)

        STEPS = B + 2

        def stage(s, off):
            return 0 <= s - off < B

        def tiles_in_use(eng):
            eng.wait_ge(experts_known, 1)
            return eng.value_load(tiles_used[0:1, 0:1], min_val=FULL * SLOTS, max_val=ST)

        block = ctx.enter_context(nc.Block())

        @block.sync
        def _(sp):
            with nc.allow_non_contiguous_dma(reason="small weights and ids"):
                sp.dma_start(ids[:, :].rearrange("p (b c) -> p b c", c=CB),
                             x.rearrange("b (p c) -> p b c", c=CB)).then_inc(ids_in, 16)
                sp.dma_start(proj_s[:, :, 0, :], proj.rearrange("(p a) r -> p a r", a=2)).then_inc(proj_in, 16)
                for n, (w, b) in enumerate(((Wv, bv), (Wk, bk), (Wq, bq))):
                    sp.dma_start(qkv[:, n, :, 0:D], w.rearrange("(p a) d -> p a d", a=2)).then_inc(qkv_in, 16)
                    sp.dma_start(qkv[:, n, :, D:D1], b.rearrange("(p a o) -> p a o", a=2, o=1)).then_inc(qkv_in, 16)
                we = We.rearrange("g d e -> d g e")
                sp.dma_start(gate_m[:, 0, :], Wg[0:P, :]).then_inc(gate_in, 16)
                sp.dma_start(gate_r[:, 0, :], Wg[P:D, :]).then_inc(gate_in, 16)
                sp.dma_start(gate_m[:, 1:C, :], we[0:P]).then_inc(gate_in, 16)
                sp.dma_start(gate_r[:, 1:C, :], we[P:D]).then_inc(gate_in, 16)
                sp.dma_start(gate_b[:, 0, :], bg.partition_broadcast(P)).then_inc(gate_in, 16)
                sp.dma_start(gate_b[:, 1:C, :], be.partition_broadcast(P)).then_inc(gate_in, 16)
                sp.dma_start(b2_s[:, :], b2.rearrange("g e d -> (g e) d")).then_inc(b2_in, 16)
                sp.dma_start(Wp_m[:, :], Wp[0:P, :]).then_inc(b2_in, 16)
                sp.dma_start(Wp_r[0:DR, :], Wp[P:D, :]).then_inc(b2_in, 16)
                sp.dma_start(Wp_r[DR + EX:DR + EX + 1, :], bp.rearrange("(a d) -> a d", a=1)).then_inc(tail_in, 16)
                sp.dma_start(gam[:, :], gamma.partition_broadcast(P)).then_inc(tail_in, 16)
                sp.dma_start(bet[:, :], beta.partition_broadcast(P)).then_inc(tail_in, 16)
            for b in range(B):
                sp.wait_ge(x2_done, b + 1)
                sp.dma_start(x_store[:, CB * b:CB * b + CB, :], x2[:, CB * b:CB * b + CB, :]).then_inc(x2_out, 16)

            sp.wait_ge(setup_ev, 4)
            sp.dma_start(Wp_r[DR:DR + EX, :], b2p[:, :]).then_inc(b2p_in, 16)

            sp.wait_ge(experts_known, 1)

            def load(t, u):
                e = sp.value_load(expert[0:1, bass.ds(t, 1)], min_val=0, max_val=EX - 1)
                sp.dma_start(W1_m[u][:, :], W1_e[bass.ds(e, 1), 0:P, :].rearrange("a d h -> (a d) h")).then_inc(w_in[u], 16)
                sp.dma_start(W1_r[u][0:DR, :], W1_e[bass.ds(e, 1), P:D, :].rearrange("a d h -> (a d) h")).then_inc(w_in[u], 16)
                sp.dma_start(W1_r[u][DR:DR + 1, :], b1_e[bass.ds(e, 1), :]).then_inc(w_in[u], 16)
                sp.dma_start(W2_s[u][:, :, :].rearrange("p j d -> p (j d)"), W2_e[bass.ds(e, 1)].rearrange("a p n -> (a p) n")).then_inc(w_in[u], 16)

            for t in range(SLOTS - 1):
                load(t, t)

            def body(t, u):
                at_least(sp, down_mm, t)
                load(t + SLOTS - 1, (u + SLOTS - 1) % SLOTS)

            for u in range(SLOTS):
                body(u, u)
            with sp.Fori(1, FULL) as i:
                for u in range(SLOTS):
                    body(i * SLOTS + u, u)
            used = tiles_in_use(sp)
            with sp.Fori(FULL, ROUNDS) as i:
                for u in range(SLOTS):
                    with sp.If(used > i * SLOTS + u):
                        body(i * SLOTS + u, u)

            for u in range(SLOTS):
                sp.wait_ge(w_in[u], (used + (2 * SLOTS - 2 - u)) // SLOTS * 64)
            sp.wait_ge(moe_done, 1)
            for b in range(B):
                sp.dma_start(ys[:, :, CB * b:CB * b + CB, :].rearrange("p k i d -> p k (i d)"),
                             y_load[:, :, CB * b:CB * b + CB, :].rearrange("k p i d -> p k (i d)")).then_inc(ys_in[b], 16)
            for b in range(B):
                sp.wait_ge(fin_done, b + 1)
                sp.dma_start(out_b[b], fin[:, CB * b:CB * b + CB, :]).then_inc(fin_out, 16)
            sp.wait_ge(fin_out, 16 * B)

        @block.gpsimd
        def _(pool):
            iota = dict(allow_small_or_imprecise_dtypes=True)
            pool.iota(diff[:, :], [[1, P]], base=0, channel_multiplier=-1, **iota).then_inc(consts, 1)
            pool.wait_ge(ids_in, 16)
            for i in range(NT):
                pool.indirect_dma_start(emb[:, i, :], None, table, bass.IndirectOffsetOnAxis(
                    ap=ids[:, i:i + 1].bitcast(U32), axis=0)).then_inc(gathered[i // CB], 16)
            pool.iota(lane[:, :], [[1, P]], base=0, channel_multiplier=0, **iota).then_inc(consts, 1)
            pool.iota(rank4[:, :], [[-1, G]], base=G, channel_multiplier=0, **iota).then_inc(consts, 1)
            pool.iota(step128[:, :], [[P, NT]], base=0, channel_multiplier=0, **iota).then_inc(consts, 1)
            pool.iota(tile_no[:, :], [[1, STP]], base=0, channel_multiplier=0, **iota).then_inc(consts, 1)
            pool.iota(row_id[:, 0, :], [[1, NT]], base=1, channel_multiplier=NT, **iota).then_inc(consts, 1)
            pool.iota(row_id[:, 1, :], [[-1, NT]], base=-1, channel_multiplier=-NT, **iota).then_inc(consts, 1)
            pool.iota(dump[:, :, :], [[0, STP // SLOTS], [P, SLOTS]], base=K * TOKENS, channel_multiplier=1, **iota).then_inc(consts, 1)
            pool.memset(inv[:, 0, ST:STP], 0.0).then_inc(consts, 1)
            pool.wait_ge(tail_in, 48)
            pool.wait_ge(x2_done, B)
            pool.tensor_tensor(h2[:, :, :], h2[:, :, :], bet[:, :].unsqueeze(1).to_broadcast([P, NT, D]),
                               ALU.add).then_inc(resid, 1)

            pool.wait_ge(ends_known, 1)
            pool.tensor_tensor(past[:, :, :], tile_no[0:1, :].unsqueeze(2).to_broadcast([1, STP, EX]),
                               end_e[0:1, :].unsqueeze(1).to_broadcast([1, STP, EX]), ALU.subtract).then_inc(pool_done, 1)
            pool.wait_ge(pool_done, 1)
            pool.tensor_scalar(past[:, :, :], past[:, :, :], 0.0, None, ALU.is_ge).then_inc(pool_done, 1)
            pool.wait_ge(pool_done, 2)
            width, steps = EX // 2, 2
            while width:
                into = past[:, :, 0:width] if width > 1 else expert_f[:, :].unsqueeze(2)
                pool.tensor_tensor(into, past[:, :, 0:width], past[:, :, width:2 * width], ALU.add).then_inc(pool_done, 1)
                steps += 1
                pool.wait_ge(pool_done, steps)
                width //= 2
            pool.tensor_scalar(expert[:, :], expert_f[:, :], float(EX - 1), None, ALU.min)
            pool.tensor_copy(tiles_used[:, :], end_e[0:1, EX - 1:EX]).then_inc(experts_known, 1)
            pool.wait_ge(slots_known, 1)
            rows = row_id[:, :, :].rearrange("p k i -> p (k i)")
            for m in range(OWN, K * NT):
                pool.tensor_scalar(hot_tile[:, m, :], lane[:, 0:ST], slot_p[:, 0, m:m + 1], rows[:, m:m + 1],
                                   ALU.is_equal, ALU.mult).then_inc(hot_t, 1)

            pool.wait_ge(routed, 1)
            pool.wait_ge(x2_out, 16 * B)

            def gather(t, u):
                pool.tensor_copy(token_i[u][:, :], token_of[:, bass.ds(t, 1)]).then_inc(token_copied, 1)
                pool.wait_ge(token_copied, t + 1)
                pool.sem_inc(pool_passed, 1)
                pool.indirect_dma_start(xg[u][:, :], None, x_rows, bass.IndirectOffsetOnAxis(
                    ap=token_i[u][:, :].bitcast(U32), axis=0)).then_inc(tok_in[u], 16)

            for t in range(SLOTS + 1):
                at_least(pool, xs_mm, t - SLOTS + 1)
                gather(t, t % SLOTS)

            def body(t, u, i):
                pool.wait_ge(xs_mm, t + 2)
                gather(t + SLOTS + 1, (u + 1) % SLOTS)
                at_least(pool, sent[u], 16 * i)
                pool.tensor_copy(dest_i[u][:, :], dest_of[:, bass.ds(t, 1)]).then_inc(dest_copied, 1)
                pool.wait_ge(dest_copied, t + 1)
                pool.wait_ge(y_ev, t + 1)
                pool.sem_inc(pool_passed, 1)
                pool.indirect_dma_start(y_rows, bass.IndirectOffsetOnAxis(
                    ap=dest_i[u][:, :].bitcast(U32), axis=0), yo[u][:, :], None).then_inc(sent[u], 16)

            for u in range(SLOTS):
                body(u, u, 0)
            with pool.Fori(1, FULL) as i:
                for u in range(SLOTS):
                    body(i * SLOTS + u, u, i)
            used = tiles_in_use(pool)
            with pool.Fori(FULL, ROUNDS) as i:
                for u in range(SLOTS):
                    with pool.If(used > i * SLOTS + u):
                        body(i * SLOTS + u, u, i)
            for u in range(SLOTS):
                pool.wait_ge(sent[u], (used + (SLOTS - 1 - u)) // SLOTS * 16)
                pool.wait_ge(tok_in[u], (used + (2 * SLOTS - u)) // SLOTS * 16)
            pool.sem_inc(moe_done, 1)
            for b in range(B):
                tiles = slice(CB * b, CB * b + CB)
                pool.wait_ge(gam_done, b + 1)
                pool.tensor_tensor(fin[:, tiles, :], fin[:, tiles, :], h2[:, tiles, :], ALU.add).then_inc(fin_done, 1)

        @block.scalar
        def _(act):
            def copy(dst, src, s=None):
                ins = nc.scalar.activation(dst, src, ACT.Copy)
                if s is not None:
                    ins.then_inc(s, 1)

            def halves(rows):
                return rows.rearrange("q (p a) -> q a p", a=2)

            def turned(rows):
                return rows.rearrange("q (a p) -> q a p", a=2)

            act.wait_ge(setup_mm, 1)
            copy(halves(projT[:, :]), turned(ps_pr), setup_ev)
            act.wait_ge(setup_mm, 2)
            copy(halves(WvT_m[:, :]), turned(ps_wm))
            copy(halves(WvT_r[:, :]), turned(ps_wr))
            nc.scalar.activation(AT_m[:, :], ps_am, ACT.Copy, scale=float(D) ** -0.5)
            nc.scalar.activation(AT_r[:, :], ps_ar, ACT.Copy, scale=float(D) ** -0.5).then_inc(setup_ev, 1)

            for s in range(STEPS):
                if stage(s, 0):
                    b = s
                    act.wait_ge(low_mm, b + 1)
                    at_least(act, h_mm, b - 1)
                    copy(lowT[:, b % 2, :], ps_low, low_ev)
                if stage(s, 1):
                    b = s - 1
                    act.wait_ge(gv_mm, b + 1)
                    at_least(act, bb_mm, b - 1)
                    copy(gv_m[:, b % 2, :], ps_vm)
                    copy(gv_r[:, b % 2, :], ps_vr, gv_ev)
                if stage(s, 0):
                    b = s
                    act.wait_ge(h_mm, b + 1)
                    for c in range(CB):
                        copy(h[:, CB * b + c, :], ps_h[c], h_ev)
                if stage(s, 2):
                    b = s - 2
                    act.wait_ge(x2T_mm, b + 1)
                    at_least(act, logits, b - 1)
                    copy(x2T_m[:, b % 2, :], ps_x2m)
                    copy(x2T_r[:, b % 2, :], ps_x2r, x2T_ev)
                if stage(s, 0):
                    act.wait_ge(var1, s + 1)
                    nc.scalar.activation(sd[:, 0, :], ve[:, 0, :], ACT.Sqrt).then_inc(sd1, 1)
                if stage(s, 1):
                    b = s - 1
                    act.wait_ge(bb_mm, b + 1)
                    at_least(act, att_mm, b - 1)
                    copy(bb_m[:, b % 2, :], ps_bm)
                    copy(bb_r[:, b % 2, :], ps_br, bb_ev)
                if stage(s, 0):
                    b = s
                    act.wait_ge(gram_mm, b + 1)
                    at_least(act, gv_mm, b - 1)
                    copy(gram_m[:, b % 2, :], ps_gm)
                    copy(gram_r[:, b % 2, :], ps_gr, gram_ev)
                    act.wait_ge(xT_mm, b + 1)
                    at_least(act, att_mm, b - 1)
                    copy(xT_m[:, b % 2, :], ps_xm)
                    copy(xT_r[:, b % 2, :], ps_xr, xT_ev)
                if stage(s, 1):
                    b = s - 1
                    act.wait_ge(var2, b + 1)
                    nc.scalar.activation(sd[:, 1, :], ve[:, 1, :], ACT.Sqrt).then_inc(sd2, 1)

            act.wait_ge(idle_set, 1)
            nc.scalar.activation(idle[:, :], idle[:, :], ACT.Exp)
            act.wait_ge(setup_mm, 3)
            copy(b2T_m[:, :], ps_2m)
            copy(b2T_r[:, :], ps_2r, setup_ev)
            act.wait_ge(setup_mm, 4)
            copy(b2p[:, :], ps_2p, setup_ev)
            act.wait_ge(lg_ready, 1)
            nc.scalar.activation(lg[:, :, :], lx[:, :, :], ACT.Exp).then_inc(lg_exp, 1)
            nc.scalar.activation(idle[:, :], idle[:, :], ACT.Gelu)

            def body(t, u):
                v = u % 2
                act.wait_ge(up_mm, t + 1)
                at_least(act, down_mm, t - 1)
                nc.scalar.activation(hT[v][:, :], pA[v][:, 0:H], ACT.Gelu).then_inc(gelu_done, 1)

            for u in range(SLOTS):
                body(u, u)
            with act.Fori(1, FULL) as i:
                for u in range(SLOTS):
                    body(i * SLOTS + u, u)
            used = tiles_in_use(act)
            with act.Fori(FULL, ROUNDS) as i:
                for u in range(SLOTS):
                    with act.If(used > i * SLOTS + u):
                        body(i * SLOTS + u, u)

            nc.scalar.activation(idle[:, :], idle[:, :], ACT.Sqrt)
            def scaled(i):
                act.wait_ge(ys_in[i // CB], 16)
                nc.scalar.activation(ys[:, 0, i, :], ys[:, 0, i, :], ACT.Copy, scale=wk[:, 0, i:i + 1]).then_inc(y1w, 1)

            def turned_mix(j):
                act.wait_ge(mixT_mm, j + 1)
                at_least(act, proj_mm, j - 1)
                copy(mixT_m[:, j % 2, :], pX[j % 2][:, 0:P])
                copy(mixT_r[:, j % 2, :], pX[j % 2][0:DR + EX + 1, P:2 * P], mixT_ev)

            for i in range(CB):
                scaled(i)
            for i in range(CB):
                scaled(CB + i)
                turned_mix(i)
            for i in range(CB):
                scaled(2 * CB + i)
                turned_mix(CB + i)
            for b in range(B):
                act.wait_ge(var3, b + 1)
                nc.scalar.activation(sd[:, 2, :], ve[:, 2, :], ACT.Sqrt).then_inc(sd3, 1)
                if b + 3 < B:
                    for c in range(CB):
                        scaled(CB * (b + 3) + c)
                if b + 2 < B:
                    turned_mix(CB * (b + 2))
                act.wait_ge(norm3, b + 1)
                for c in range(CB):
                    nc.scalar.activation(fin[:, CB * b + c, :], ps_y[b % 3][c], ACT.Identity, bias=nm[:, c:c + 1],
                                         scale=rs[:, 2, c:c + 1]).then_inc(z_done, 1)
                if b + 2 < B:
                    turned_mix(CB * (b + 2) + 1)

        @block.vector
        def _(dve):
            made = [0]

            def link(ins):
                made[0] += 1
                ins.then_inc(dve_done, 1)
                dve.wait_ge(dve_done, made[0])

            nc.vector.memset(ones[:, :], 1.0)
            nc.vector.memset(carry[:, :, :], 1.0)
            nc.vector.memset(unit[:, :], 1.0)
            nc.vector.memset(idle[:, :], 1.0).then_inc(idle_set, 1)
            nc.vector.memset(x2[:, :, D:ROW], 1.0)
            nc.vector.memset(mixw[:, :, D + EX:D + EX + 1], 1.0)
            link(nc.vector.memset(xh[:, :, :, D:D1], 1.0))
            nc.vector.memset(carry[:, :, 0:1], 0.0)
            dve.wait_ge(consts, 1)
            nc.vector.tensor_scalar(ident[:, :], diff[:, :], 0.0, None, ALU.is_equal).then_inc(masks, 1)
            dve.wait_ge(proj_in, 16)
            nc.vector.tensor_copy(proj_s[:, :, 1, :], proj_s[:, :, 0, :]).then_inc(proj_twice, 1)
            nc.vector.tensor_scalar(before[:, :], diff[:, :], 0.0, None, ALU.is_gt).then_inc(masks, 1)

            def root_input(n, ready):
                nc.vector.tensor_scalar(ve[:, n, :], mv[:, n, :, 1], EPS, 0.25, ALU.add, ALU.mult).then_inc(ready, 1)

            def newton(n):
                for c in range(CB):
                    ins = nc.vector.tensor_scalar(tn[:, n, c:c + 1], rs[:, n, c:c + 1], ve[:, n, c:c + 1],
                                                  sd[:, n, c:c + 1], ALU.mult, ALU.add)
                return ins

            def rsqrt(n, ready, root, count):
                root_input(n, ready)
                dve.wait_ge(root, count)
                link(nc.vector.reciprocal(rs[:, n, :], sd[:, n, :]))
                link(newton(n))
                link(nc.vector.reciprocal(rs[:, n, :], tn[:, n, :]))

            for s in range(STEPS):
                if stage(s, 0):
                    b = s
                    for c in range(CB):
                        dve.wait_ge(h_ev, CB * b + c + 1)
                        ins = nc.vector.bn_stats(stats[:, 0, c, :], h[:, CB * b + c, :])
                    link(ins)
                    nc.vector.bn_aggr(mv[:, 0, 0, :], stats[:, 0, 0, :])
                    link(nc.vector.bn_aggr(mv[:, 0, 1, :], stats[:, 0, 1, :]))
                    rsqrt(0, var1, sd1, b + 1)
                    at_least(dve, xT_mm, b - 1)
                    for c in range(CB):
                        ins = nc.vector.tensor_scalar(xh[:, b % 2, c, 0:D], h[:, CB * b + c, :], mv[:, 0, c, 0:1],
                                                      rs[:, 0, c:c + 1], ALU.subtract, ALU.mult)
                    ins.then_inc(h_norm, 1)
                if stage(s, 1):
                    b = s - 1
                    tiles = slice(CB * b, CB * b + CB)
                    dve.wait_ge(att_mm, b + 1)
                    nc.vector.tensor_tensor(h2[:, tiles, :], ps_o, h[:, tiles, :], ALU.add).then_inc(h2_done, 1)
                    dve.wait_ge(h2_done, b + 1)
                    for c in range(CB):
                        ins = nc.vector.bn_stats(stats[:, 1, c, :], h2[:, CB * b + c, :])
                    link(ins)
                    for c in range(CB):
                        ins = nc.vector.bn_aggr(mv[:, 1, c, :], stats[:, 1, c, :])
                    link(ins)
                    rsqrt(1, var2, sd2, b + 1)
                    for c in range(CB):
                        ins = nc.vector.tensor_scalar(x2[:, CB * b + c, 0:D], h2[:, CB * b + c, :], mv[:, 1, c, 0:1],
                                                      rs[:, 1, c:c + 1], ALU.subtract, ALU.mult)
                    ins.then_inc(x2_done, 1)

            V = nc.vector
            dve.wait_ge(logits, B)
            dve.wait_ge(gate_in, 96)
            dve.wait_ge(consts, 9)
            N = NT * C
            lg_v = lg[:, :, :].rearrange("p (i c) e -> p i (c e)", c=C)
            link(V.tensor_tensor(lg_v, ps_lg.rearrange("p (i n) -> p i n", i=NT),
                                 gate_b[:, :, :].rearrange("p c e -> p (c e)").unsqueeze(1).to_broadcast([P, NT, 4 * C]),
                                 ALU.add))
            link(V.tensor_reduce(r4[:, :], lg[:, :, :], AX.X, ALU.max))
            V.tensor_tensor(lx[:, :, :], lg[:, :, :], r4[:, :].unsqueeze(2).to_broadcast([P, N, 4]),
                            ALU.subtract).then_inc(lg_ready, 1)
            dve.wait_ge(lg_exp, 1)
            link(V.tensor_reduce(r4[:, :], lg[:, :, :], AX.X, ALU.add))
            link(V.reciprocal(r4[:, :], r4[:, :]))
            pr_v = pr[:, :, :, :].rearrange("p i c e -> p (i c) e")
            link(V.tensor_tensor(pr_v, lg[:, :, :], r4[:, :].unsqueeze(2).to_broadcast([P, N, 4]), ALU.mult))

            def top(chosen, best, prob, n, keys, kbest):
                link(V.tensor_reduce(best, prob, AX.X, ALU.max))
                link(V.tensor_tensor(chosen, prob, best.unsqueeze(2).to_broadcast([P, n, 4]), ALU.is_equal))
                link(V.tensor_tensor(keys, chosen, rank4[:, :].unsqueeze(1).to_broadcast([P, n, 4]), ALU.mult))
                link(V.tensor_reduce(kbest, keys, AX.X, ALU.max))
                link(V.tensor_tensor(chosen, keys, kbest.unsqueeze(2).to_broadcast([P, n, 4]), ALU.is_equal))

            top(first[:, :, :, :].rearrange("p i c e -> p (i c) e"), pmax[:, :, :].rearrange("p i c -> p (i c)"),
                pr_v, N, key[:, :, :], kmax[:, :])
            link(V.scalar_tensor_tensor(out=pg2[:, :, :], in0=first[:, :, 0, :], scalar=-4.0, in1=pr[:, :, 0, :],
                                        op0=ALU.mult, op1=ALU.add))
            top(second[:, :, :], gmax2[:, :], pg2[:, :, :], NT, key[:, 0:NT, :], kmax[:, 0:NT])
            groups = (first[:, :, 0, :], second[:, :, :])
            gws = (pmax[:, :, 0], gmax2[:, :])
            for k in range(K):
                ins = V.tensor_tensor(sel[:, k, :, :].rearrange("p i (g e) -> p i g e", g=G),
                                      groups[k].unsqueeze(3).to_broadcast([P, NT, G, E]),
                                      first[:, :, 1:C, :], ALU.mult)
            link(ins)
            V.tensor_tensor(both[:, :, :], sel[:, 0, :, :], sel[:, 1, :, :], ALU.add).then_inc(picked, 1)
            for k in range(K):
                link(V.tensor_tensor(wg_[:, :, :], groups[k], pmax[:, :, 1:C], ALU.mult))
                link(V.tensor_reduce(wk[:, k, :], wg_[:, :, :], AX.X, ALU.add))
                link(V.tensor_tensor(wk[:, k, :], wk[:, k, :], gws[k], ALU.mult))
            dve.wait_ge(counted, 1)
            link(V.tensor_copy(total[:, :, :], ps_tot.rearrange("p i e -> p e i")))
            link(V.tensor_tensor_scan(upto[:, :, :].rearrange("p e i -> p (e i)"),
                                      carry[:, :, :].rearrange("p e i -> p (e i)"),
                                      total[:, :, :].rearrange("p e i -> p (e i)"), 0.0, ALU.mult, ALU.add))
            link(V.tensor_tensor(more[:, :, :], upto[:, :, NT - 1:NT].to_broadcast([P, EX, NT]),
                                 step128[:, :].unsqueeze(1).to_broadcast([P, EX, NT]), ALU.is_gt))
            link(V.tensor_reduce(tiles_e[:, :], more[:, :, :], AX.X, ALU.add))
            link(V.tensor_tensor_scan(end_e[:, :], unit[:, :], tiles_e[:, :], 0.0, ALU.mult, ALU.add))
            link(V.tensor_tensor(base_e[:, :], end_e[:, :], tiles_e[:, :], ALU.subtract))
            V.tensor_scalar(base_e[:, :], base_e[:, :], float(P), None, ALU.mult).then_inc(ends_known, 1)
            dve.wait_ge(ends_known, 1)
            link(V.tensor_tensor(upto[:, :, :], upto[:, :, :], total[:, :, :], ALU.subtract))
            link(V.tensor_tensor(upto[:, :, :], upto[:, :, :], base_e[:, :].unsqueeze(2).to_broadcast([P, EX, NT]), ALU.add))
            link(V.tensor_tensor(place[:, :, :], ps_rank, upto[:, :, :].rearrange("p e i -> p i e"), ALU.add))
            link(V.tensor_tensor(placed[:, :, :, :], sel[:, :, :, :],
                                 place[:, :, :].unsqueeze(1).to_broadcast([P, K, NT, EX]), ALU.mult))
            link(V.tensor_reduce(slot_f[:, :], placed[:, :, :, :].rearrange("p k i e -> p (k i) e"), AX.X, ALU.add))
            link(V.tensor_copy(slot_i[:, :], slot_f[:, :]))
            V.tensor_scalar(slot_t[:, 0, :], slot_i[:, :], 7, None, ALU.arith_shift_right)
            link(V.tensor_scalar(slot_t[:, 1, :], slot_i[:, :], P - 1, None, ALU.bitwise_and))
            V.tensor_copy(slot_p[:, :, :], slot_t[:, :, :]).then_inc(slots_known, 1)
            dve.wait_ge(slots_known, 1)
            rows = row_id[:, :, :].rearrange("p k i -> p (k i)")
            for q in range(0, K * NT, 8):
                ms = slice(q, q + 8)
                if q < OWN:
                    link(V.tensor_tensor(hot_tile[:, ms, :], lane[:, 0:ST].unsqueeze(1).to_broadcast([P, 8, ST]),
                                         slot_p[:, 0, ms].unsqueeze(2).to_broadcast([P, 8, ST]), ALU.is_equal))
                    V.tensor_tensor(hot_tile[:, ms, :], hot_tile[:, ms, :],
                                    rows[:, ms].unsqueeze(2).to_broadcast([P, 8, ST]), ALU.mult)
                for m in range(q, q + 8):
                    V.tensor_scalar(hot_lane[:, m, :], lane[:, :], slot_p[:, 1, m:m + 1], None, ALU.is_equal).then_inc(hot, 1)
            dve.wait_ge(inv_mm, 1)
            link(V.tensor_copy(inv[:, 0, 0:ST], ps_inv))
            V.tensor_scalar(inv[:, 1, :], inv[:, 0, :], 0.0, float(TOKENS), ALU.is_lt, ALU.mult)
            link(V.tensor_scalar(inv[:, 2, :], inv[:, 0, :], -1.0, None, ALU.mult))
            link(V.tensor_tensor(inv[:, 2, :], inv[:, 2, :], inv[:, 0, :], ALU.max))
            V.tensor_scalar(inv[:, 3, :], inv[:, 2, :], 0.5, None, ALU.is_gt)
            link(V.tensor_scalar(inv[:, 2, :], inv[:, 2, :], -1.0, 0.0, ALU.add, ALU.max))
            V.tensor_copy(token_of[:, :], inv[:, 2, :])
            link(V.tensor_tensor(inv[:, 4, :], inv[:, 2, :], inv[:, 1, :], ALU.add))
            spare = dump[:, :, :].rearrange("p a b -> p (a b)")
            link(V.tensor_tensor(inv[:, 5, :], inv[:, 4, :], spare, ALU.subtract))
            link(V.tensor_tensor(inv[:, 5, :], inv[:, 5, :], inv[:, 3, :], ALU.mult))
            V.tensor_tensor(dest_of[:, :], inv[:, 5, :], spare, ALU.add).then_inc(routed, 1)
            for k in range(K):
                V.tensor_tensor(placed[:, k, :, :], sel[:, k, :, :],
                                wk[:, k, :].unsqueeze(2).to_broadcast([P, NT, EX]), ALU.mult)
            link(V.tensor_copy(wsel[:, :, :], sel[:, 0, :, :]))
            link(V.tensor_tensor(mixw[:, :, D:D + EX], placed[:, 0, :, :], placed[:, 1, :, :], ALU.add))

            def turned(t, v):
                dve.wait_ge(xs_mm, t + 1)
                at_least(dve, up_mm, t - 1)
                V.tensor_copy(xs_m[v][:, :], pX[v][:, 0:P])
                V.tensor_copy(xs_r[v][:, :], pX[v][0:DR + 1, P:2 * P]).then_inc(xs_ev, 1)

            turned(0, 0)
            turned(1, 1)

            def body(t, u, i):
                v = u % 2
                turned(t + 2, v)
                dve.wait_ge(down_mm, t + 1)
                at_least(dve, sent[u], 16 * i)
                V.tensor_copy(yo[u][:, :], pY[v][:, 0:D]).then_inc(y_ev, 1)

            for u in range(SLOTS):
                body(u, u, 0)
            with dve.Fori(1, FULL) as i:
                for u in range(SLOTS):
                    body(i * SLOTS + u, u, i)
            used = tiles_in_use(dve)
            with dve.Fori(FULL, ROUNDS) as i:
                for u in range(SLOTS):
                    with dve.If(used > i * SLOTS + u):
                        body(i * SLOTS + u, u, i)

            dve.wait_ge(resid, 1)

            def times_gamma(b):
                dve.wait_ge(z_done, CB * b + CB)
                tiles = slice(CB * b, CB * b + CB)
                V.tensor_tensor(fin[:, tiles, :], fin[:, tiles, :], gam[:, :].unsqueeze(1).to_broadcast([P, CB, D]),
                                ALU.mult).then_inc(gam_done, 1)

            def mix(i):
                dve.wait_ge(y1w, i + 1)
                V.scalar_tensor_tensor(out=mixw[:, i, 0:D], in0=ys[:, 1, i, :], scalar=wk[:, 1, i:i + 1],
                                       in1=ys[:, 0, i, :], op0=ALU.mult, op1=ALU.add).then_inc(mix_done, 1)

            for i in range(2 * CB):
                mix(i)
            for b in range(B):
                for c in range(CB):
                    dve.wait_ge(proj_mm, CB * b + c + 1)
                    ins = V.bn_stats(stats[:, 0, c, :], ps_y[b % 3][c])
                link(ins)
                for c in range(CB):
                    ins = V.bn_aggr(mv[:, 2, c, :], stats[:, 0, c, :])
                link(ins)
                root_input(2, var3)
                if b >= 1:
                    times_gamma(b - 1)
                dve.wait_ge(sd3, b + 1)
                V.reciprocal(rs[:, 2, :], sd[:, 2, :]).then_inc(root_step, 1)
                if b + 2 < B:
                    mix(CB * (b + 2))
                dve.wait_ge(root_step, 3 * b + 1)
                newton(2).then_inc(root_step, 1)
                if b + 2 < B:
                    mix(CB * (b + 2) + 1)
                dve.wait_ge(root_step, 3 * b + 2)
                V.reciprocal(rs[:, 2, :], tn[:, 2, :]).then_inc(root_step, 1)
                dve.wait_ge(root_step, 3 * b + 3)
                V.scalar_tensor_tensor(out=nm[:, :], in0=mv[:, 2, :, 0], scalar=-1.0, in1=rs[:, 2, :],
                                       op0=ALU.mult, op1=ALU.mult).then_inc(norm3, 1)
            times_gamma(B - 1)

        @block.tensor
        def _(pe):
            def two(out_ap, m_l, m_r, r_l, r_r):
                pe.matmul(out_ap, m_l, r_l, start=True, stop=False)
                return pe.matmul(out_ap, m_r, r_r, start=False, stop=True)

            pe.wait_ge(masks, 2)
            half = ident[0:D // 2, 0:D // 2]
            pe.wait_ge(proj_twice, 1)
            for a in range(2):
                mm = pe.transpose(ps_pr[:, a * D // 2:(a + 1) * D // 2],
                                  proj_s[:, a, :, :].rearrange("p c r -> p (c r)"), half)
            mm.then_inc(setup_mm, 1)
            pe.wait_ge(qkv_in, 16 * 6)
            for a in range(2):
                pe.transpose(ps_wm[:, a * D // 2:(a + 1) * D // 2], qkv[:, 0, a, 0:P], half)
                pe.transpose(ps_wr[:, a * D // 2:(a + 1) * D // 2], qkv[:, 0, a, P:D1], half)
            two(ps_am, qkv[:, 1, 0, 0:P], qkv[:, 1, 1, 0:P], qkv[:, 2, 0, :], qkv[:, 2, 1, :])
            two(ps_ar, qkv[:, 1, 0, P:D1], qkv[:, 1, 1, P:D1], qkv[:, 2, 0, :], qkv[:, 2, 1, :]).then_inc(setup_mm, 1)
            pe.wait_ge(setup_ev, 2)

            for s in range(STEPS):
                if stage(s, 0):
                    b = s
                    pe.wait_ge(gathered[b], 16 * CB)
                    at_least(pe, low_ev, b)
                    pe.transpose(ps_low, emb[:, CB * b:CB * b + CB, :].rearrange("p c r -> p (c r)"),
                                 ident[:, :]).then_inc(low_mm, 1)
                if stage(s, 1):
                    b = s - 1
                    q = b % 2
                    pe.wait_ge(gram_ev, b + 1)
                    at_least(pe, gv_ev, b)
                    two(ps_vm, gram_m[:, q, 0:P], gram_r[:, q, 0:P], WvT_m[:, :], WvT_r[:, :])
                    two(ps_vr, gram_m[:, q, P:D1], gram_r[:, q, P:D1], WvT_m[:, :], WvT_r[:, :]).then_inc(gv_mm, 1)
                if stage(s, 0):
                    b = s
                    pe.wait_ge(low_ev, b + 1)
                    at_least(pe, h_ev, CB * b)
                    for c in range(CB):
                        mm = pe.matmul(ps_h[c], lowT[c * RANK:(c + 1) * RANK, b % 2, :],
                                       projT[c * RANK:(c + 1) * RANK, :], start=True, stop=True)
                    mm.then_inc(h_mm, 1)
                if stage(s, 2):
                    b = s - 2
                    pe.wait_ge(x2_done, b + 1)
                    pe.wait_ge(xT_ev, min(b + 2, B))
                    for c in range(CB):
                        pe.transpose(ps_x2m[:, c * P:(c + 1) * P], x2[:, CB * b + c, 0:P], ident[:, :])
                        mm = pe.transpose(ps_x2r[:, c * P:(c + 1) * P], x2[:, CB * b + c, P:D], ident[:, :])
                    mm.then_inc(x2T_mm, 1)
                if stage(s, 1):
                    b = s - 1
                    q = b % 2
                    pe.wait_ge(gv_ev, b + 1)
                    at_least(pe, bb_ev, b)
                    two(ps_bm, AT_m[:, 0:P], AT_r[:, 0:P], gv_m[:, q, :], gv_r[:, q, :])
                    two(ps_br, AT_m[:, P:D1], AT_r[:, P:D1], gv_m[:, q, :], gv_r[:, q, :]).then_inc(bb_mm, 1)
                if stage(s, 2):
                    b = s - 2
                    if b == 0:
                        pe.wait_ge(gate_in, 96)
                    pe.wait_ge(x2T_ev, b + 1)
                    for c in range(CB):
                        i = CB * b + c
                        mm = two(ps_lg[:, i * 4 * C:(i + 1) * 4 * C], x2T_m[:, b % 2, c * P:(c + 1) * P],
                                 x2T_r[:, b % 2, c * P:(c + 1) * P],
                                 gate_m[:, :, :].rearrange("p c e -> p (c e)"), gate_r[:, :, :].rearrange("p c e -> p (c e)"))
                    mm.then_inc(logits, 1)
                if stage(s, 1):
                    b = s - 1
                    q = b % 2
                    pe.wait_ge(bb_ev, b + 1)
                    pe.wait_ge(xT_ev, b + 1)
                    at_least(pe, h2_done, b)
                    for c in range(CB):
                        mm = two(ps_o[:, c, :], xT_m[:, q, c * P:(c + 1) * P], xT_r[:, q, c * P:(c + 1) * P],
                                 bb_m[:, q, :], bb_r[:, q, :])
                    mm.then_inc(att_mm, 1)
                if stage(s, 0):
                    b = s
                    q = b % 2
                    pe.wait_ge(h_norm, b + 1)
                    at_least(pe, gram_ev, b)
                    for rows, lo, hi in ((ps_gm, 0, P), (ps_gr, P, D1)):
                        for c in range(CB):
                            mm = pe.matmul(rows, xh[:, q, c, lo:hi], xh[:, q, c, :], start=(c == 0), stop=(c == CB - 1))
                    mm.then_inc(gram_mm, 1)
                    at_least(pe, x2T_ev, b - 1)
                    for c in range(CB):
                        pe.transpose(ps_xm[:, c * P:(c + 1) * P], xh[:, q, c, 0:P], ident[:, :])
                        mm = pe.transpose(ps_xr[:, c * P:(c + 1) * P], xh[:, q, c, P:D1], ident[:, :])
                    mm.then_inc(xT_mm, 1)

            pe.wait_ge(b2_in, 48)
            pe.wait_ge(bb_ev, B)
            pe.transpose(ps_2m, b2_s[:, 0:P], ident[0:EX, 0:EX])
            pe.transpose(ps_2r, b2_s[:, P:D], ident[0:EX, 0:EX]).then_inc(setup_mm, 1)
            pe.wait_ge(setup_ev, 3)
            pe.wait_ge(h2_done, B)
            two(ps_2p, b2T_m[:, :], b2T_r[:, :], Wp_m[:, :], Wp_r[0:DR, :]).then_inc(setup_mm, 1)

            pe.wait_ge(picked, 1)
            chosen = both[:, :, :].rearrange("p i e -> p (i e)")
            pe.matmul(ps_rank.rearrange("p i e -> p (i e)"), before[:, :], chosen, start=True, stop=True)
            pe.matmul(ps_tot.rearrange("p i e -> p (i e)"), ones[:, :], chosen, start=True, stop=True).then_inc(counted, 1)
            for m in range(K * NT):
                if m == 0:
                    pe.wait_ge(setup_ev, 4)
                pe.wait_ge(hot, m + 1)
                at_least(pe, hot_t, m + 1 - OWN)
                mm = pe.matmul(ps_inv, hot_lane[:, m, :], hot_tile[:, m, :], start=(m == 0), stop=(m == K * NT - 1))
            mm.then_inc(inv_mm, 1)

            def turn(t, u, loads):
                v = u % 2
                pe.wait_ge(tok_in[u], loads)
                at_least(pe, xs_ev, t - 1)
                pe.transpose(pX[v][:, 0:P], xg[u][:, 0:P], ident[:, :])
                pe.transpose(pX[v][0:DR + 1, P:2 * P], xg[u][:, P:D1], ident[:, :]).then_inc(xs_mm, 1)

            def up(t, u, loads):
                v = u % 2
                pe.wait_ge(xs_ev, t + 1)
                pe.wait_ge(w_in[u], loads)
                at_least(pe, gelu_done, t - 1)
                for j in range(HC):
                    mm = two(pA[v][:, j * P:(j + 1) * P], W1_m[u][:, j::HC], W1_r[u][:, j::HC], xs_m[v][:, :], xs_r[v][:, :])
                mm.then_inc(up_mm, 1)

            def down(t, u):
                v = u % 2
                pe.wait_ge(gelu_done, t + 1)
                at_least(pe, y_ev, t - 1)
                for j in range(HC):
                    mm = pe.matmul(pY[v][:, 0:D], hT[v][:, j * P:(j + 1) * P], W2_s[u][:, j, :],
                                   start=(j == 0), stop=(j == HC - 1))
                mm.then_inc(down_mm, 1)

            turn(0, 0, 16)
            turn(1, 1, 16)
            up(0, 0, 64)

            def body(t, u, i):
                turn(t + 2, (u + 2) % SLOTS, 16 * (i + (2 if u >= SLOTS - 2 else 1)))
                up(t + 1, (u + 1) % SLOTS, 64 * (i + (2 if u == SLOTS - 1 else 1)))
                down(t, u)

            for u in range(SLOTS):
                body(u, u, 0)
            with pe.Fori(1, FULL) as i:
                for u in range(SLOTS):
                    body(i * SLOTS + u, u, i)
            used = tiles_in_use(pe)
            with pe.Fori(FULL, ROUNDS) as i:
                for u in range(SLOTS):
                    with pe.If(used > i * SLOTS + u):
                        body(i * SLOTS + u, u, i)

            for i in range(NT + 1):
                if i < NT:
                    pe.wait_ge(mix_done, i + 1)
                    at_least(pe, mixT_ev, i - 1)
                    pe.transpose(pX[i % 2][:, 0:P], mixw[:, i, 0:P], ident[:, :])
                    pe.transpose(pX[i % 2][0:DR + EX + 1, P:2 * P], mixw[:, i, P:D + EX + 1], ident[:, :]).then_inc(mixT_mm, 1)
                if i >= 1:
                    j = i - 1
                    if j == 0:
                        pe.wait_ge(b2p_in, 16)
                        pe.wait_ge(tail_in, 48)
                    pe.wait_ge(mixT_ev, j + 1)
                    at_least(pe, z_done, CB * (j // CB - 2))
                    two(ps_y[j // CB % 3][j % CB], mixT_m[:, j % 2, :], mixT_r[:, j % 2, :], Wp_m[:, :], Wp_r[:, :]).then_inc(proj_mm, 1)


_INS = ["x", "L0_tok_embed_table", "L0_tok_proj_up", "L0_attn_Wq", "L0_attn_bq", "L0_attn_Wk", "L0_attn_bk", "L0_attn_Wv",
        "L0_attn_bv", "L0_ffn_Wg", "L0_ffn_bg", "L0_ffn_We", "L0_ffn_be", "L0_ffn_W1", "L0_ffn_b1", "L0_ffn_W2",
        "L0_ffn_b2", "L0_ffn_Wp", "L0_ffn_bp", "L0_ffn_gamma", "L0_ffn_beta"]


def kernel(**inputs):
    import concourse.bacc as _bacc
    from concourse.bass_utils import run_bass_kernel_spmd as _run

    nc = _bacc.Bacc("TRN2", target_bir_lowering=False, num_devices=1)
    arrays, args = {}, []
    for name in _INS:
        a = np.ascontiguousarray(inputs[name])
        arrays[f"in_{name}_dram"] = a
        args.append(nc.dram_tensor(f"in_{name}_dram", a.shape, mybir.dt.from_np(a.dtype), kind="ExternalInput").ap())
    shape = (*inputs["x"].shape, inputs["L0_tok_proj_up"].shape[0])
    out = nc.dram_tensor("out_0_dram", shape, F32, kind="ExternalOutput").ap()
    lm_tower(nc, *args, out)
    r = _run(nc, [arrays], core_ids=[0])
    return r.results[0]["out_0_dram"]
```

```python
from contextlib import ExitStack

import numpy as np

import concourse.bass as bass
from concourse import mybir

F32 = mybir.dt.float32
F16 = mybir.dt.float16
BF16 = mybir.dt.bfloat16
I32 = mybir.dt.int32
U32 = mybir.dt.uint32
ALU = mybir.AluOpType
ACT = mybir.ActivationFunctionType
AX = mybir.AxisListType

P = 128
EPS = 1e-5


def at_least(eng, sem, count):
    if isinstance(count, int) and count <= 0:
        return
    eng.wait_ge(sem, count)


def lm_tower(nc, x, table, proj, Wq, bq, Wk, bk, Wv, bv, Wg, bg, We, be, W1, b1, W2, b2, Wp, bp, gamma, beta, out):
    B, S = x.shape
    VOCAB, RANK = table.shape
    D = proj.shape[0]
    G, E = We.shape[0], We.shape[2]
    H = W1.shape[3]
    NT = B * S // P
    TOKENS = NT * P
    CB = S // P
    DR = D - P
    D1 = D + 1
    R1 = RANK + 1
    DL = D + 4 * (1 + G)
    EX = G * E
    K = 2
    HC = H // P
    C = 1 + G
    SLOTS = 4
    ROUNDS = -(-(K * TOKENS // P + EX - 1) // SLOTS)
    ST = ROUNDS * SLOTS
    STP = ST + 2 * SLOTS
    GROUP = 8
    BUSY = 9
    LATE = 3
    EARLY = (B - LATE) * CB
    FULL = K * TOKENS // P // SLOTS
    AHEAD = (FULL + 1) * SLOTS - 1
    assert (CB, RANK, K) == (2, 64, 2) and HC * P == H and S == CB * P

    ROW = 200
    x_rows = nc.dram_tensor("x_rows", [TOKENS, ROW], F32).ap()
    y_rows = nc.dram_tensor("y_rows", [K * TOKENS + SLOTS * P, D], F32).ap()

    with ExitStack() as ctx:
        def sb(name, shape, dt=F32):
            return ctx.enter_context(nc.sbuf_tensor(name, shape, dt))

        def sem(name):
            return ctx.enter_context(nc.semaphore(name))

        diff = sb("diff", [P, P])
        ident = sb("ident", [P, P])
        before = sb("before", [P, P], BF16)
        ones = sb("ones", [P, P], BF16)
        lane = sb("lane", [P, P], F16)
        rank4 = sb("rank4", [P, G])
        step_i = sb("step_i", [P, 3], I32)
        step_f = sb("step_f", [P, 2])
        later = sb("later", [P, SLOTS - 1])
        fill = sb("fill", [P, SLOTS - 1])
        carry = sb("carry", [P, EX, NT])
        row_id = sb("row_id", [P, K, NT])
        dump = sb("dump", [P, ROUNDS, SLOTS])
        ids = sb("ids", [P, NT], I32)
        proj_s = sb("proj_s", [D // 2, 2, 2, RANK])
        projT = sb("projT", [P, D])
        PcT = sb("PcT", [P, CB, D])
        PT = sb("PT", [P, CB, DL])
        Pc = sb("Pc", [D // 2, 2, RANK])
        pmean = sb("pmean", [P, 8])
        mean_w = sb("mean_w", [D // 2, D // 2])
        vkq = sb("vkq", [D // 2, 3, 2, D1])
        vkqT = sb("vkqT", [D // 2, 3, 2, D])
        vkqc = sb("vkqc", [D // 2, 3, 2, R1])
        M1T = sb("M1T", [P, R1])
        M2 = sb("M2", [P, DL])
        gates = sb("gates", [D // 2, 2, C, 4])
        gates_c = sb("gates_c", [D // 2, 2, 4 * C])
        gate_b = sb("gate_b", [P, C, 4])
        Wp_m = sb("Wp_m", [P, D])
        Wp_r = sb("Wp_r", [DR + EX + 1, D])
        b2_s = sb("b2_s", [EX, D])
        b2T_m = sb("b2T_m", [P, EX])
        b2T_r = sb("b2T_r", [DR, EX])
        b2p = sb("b2p", [EX, D])
        gam = sb("gam", [P, D])
        bet = sb("bet", [P, D])
        emb = sb("emb", [P, NT, RANK])
        lowT = sb("lowT", [P, B, P])
        h2 = sb("h2", [P, NT, D])
        lh = sb("lh", [P, 2, CB, R1])
        lT = sb("lT", [P, 2, CB * P])
        gram = sb("gram", [P, 2, R1])
        gv = sb("gv", [P, 2, DL])
        bb = sb("bb", [P, 2, DL])
        x2 = sb("x2", [P, NT, ROW])
        raw = sb("raw", [P, NT, 4 * C])
        mu2, rs2 = sb("mu2", [P, NT]), sb("rs2", [P, NT])
        stats = sb("stats", [P, 2, CB, 6])
        mv = sb("mv", [P, 3 + LATE, CB, 2])
        ve = sb("ve", [P, 3 + LATE, CB])
        sd = sb("sd", [P, 3 + LATE, CB])
        rs = sb("rs", [P, 3 + LATE, CB])
        tn = sb("tn", [P, 3 + LATE, CB])
        lg = sb("lg", [P, NT * C, 4])
        runs_known, steps_known, pos_step = (sem(n) for n in ("runs_known", "steps_known", "pos_step"))
        rows_done = sem("rows_done")
        hot_own, hot_row = sem("hot_own"), sem("hot_row")
        experts_counted, experts_mm, tokens_known = (sem(n) for n in (
            "experts_counted", "experts_mm", "tokens_known"))
        lx = sb("lx", [P, NT * C, 4])
        r4 = sb("r4", [P, NT * C])
        pr = sb("pr", [P, NT, C, 4])
        pmax = sb("pmax", [P, NT, C])
        first = sb("first", [P, NT, C, 4])
        pr_v, first_v = (a[:, :, :, :].rearrange("p i c e -> p (i c) e") for a in (pr, first))
        pmax_v = pmax[:, :, :].rearrange("p i c -> p (i c)")
        key = sb("key", [P, NT * C, 4])
        kmax = sb("kmax", [P, NT * C])
        pg2 = sb("pg2", [P, NT, G])
        second = sb("second", [P, NT, G])
        gmax2 = sb("gmax2", [P, NT])
        sel = sb("sel", [P, K, NT, EX])
        both = sb("both", [P, NT, EX], BF16)
        wg_ = sb("wg_", [P, NT, G])
        wk = sb("wk", [P, K, NT])
        upto = sb("upto", [P, EX, NT])
        count_i = sb("count_i", [P, 2, EX], I32)
        tiles_e = sb("tiles_e", [P, EX])
        end_e = sb("end_e", [P, EX])
        unit = sb("unit", [P, EX])
        base_e = sb("base_e", [P, EX])
        run_i = sb("run_i", [P, 2, SLOTS - 1], I32)
        run = sb("run", [P, SLOTS - 1])
        run_end = sb("run_end", [P, SLOTS - 1])
        run_step = sb("run_step", [P, SLOTS - 1])
        skipped = sb("skipped", [P, SLOTS - 1])
        tile_of = sb("tile_of", [P, 1])
        beyond = sb("beyond", [P, SLOTS - 1, K * NT])
        moved = sb("moved", [P, K * NT])
        slot_h = sb("slot_h", [P, K * NT], F16)
        step_h = sb("step_h", [P, K * NT], F16)
        rows_h = sb("rows_h", [P, K * NT], F16)
        past = sb("past", [P, EX])
        expert_f = sb("expert_f", [P, 1])
        expert = sb("expert", [1, STP], I32)
        tiles_used = sb("tiles_used", [1, 1], I32)
        steps_loaded = sb("steps_loaded", [1, 1], I32)
        place = sb("place", [P, NT, EX])
        placed = sb("placed", [P, K, NT, EX])
        slot_f = sb("slot_f", [P, K * NT])
        slot_i = sb("slot_i", [P, K * NT], I32)
        slot_t = sb("slot_t", [P, 2, K * NT], I32)
        slot_p = sb("slot_p", [P, 2, K * NT])
        inv = sb("inv", [P, 4, ST])
        token_of = sb("token_of", [P, STP], I32)
        dest_of = sb("dest_of", [P, ST], I32)
        mixw = sb("mixw", [P, NT, D + EX + 1])
        wsel = sb("wsel", [P, NT, EX])
        token_i = [sb(f"token_i{u}", [P, 1], I32) for u in range(SLOTS)]
        dest_i = [sb(f"dest_i{u}", [P, 1], I32) for u in range(SLOTS)]
        xg = [sb(f"xg{u}", [P, ROW]) for u in range(SLOTS)]
        xs_m = [sb(f"xs_m{u}", [P, P]) for u in range(2)]
        xs_r = [sb(f"xs_r{u}", [DR + 1, P]) for u in range(2)]
        W1_m = [sb(f"W1_m{u}", [P, H]) for u in range(SLOTS)]
        W1_r = [sb(f"W1_r{u}", [DR + 1, H]) for u in range(SLOTS)]
        W2_s = [sb(f"W2_s{u}", [P, HC, D]) for u in range(SLOTS)]
        hT = [sb(f"hT{u}", [P, H]) for u in range(2)]
        yo = [sb(f"yo{u}", [P, D]) for u in range(SLOTS)]
        ys = sb("ys", [P, K, NT, D])
        room = ys[:, 0, :, :].rearrange("p i d -> p (i d)").bitcast(F16)
        hot_lane = room[:, 0:K * NT * P].rearrange("p (m l) -> p m l", l=P)
        hot_tile = room[:, K * NT * P:K * NT * (P + ST)].rearrange("p (m t) -> p m t", t=ST)
        mixT_m = sb("mixT_m", [P, 2, P])
        mixT_r = sb("mixT_r", [DR + EX + 1, 2, P])
        nm = sb("nm", [P, CB])
        idle = sb("idle", [P, 8])
        fin = ys[:, 0, :, :]

        pA = [ctx.enter_context(nc.psum_tensor(f"pA{u}", [P, 1024], F32)) for u in range(2)]
        pX = [ctx.enter_context(nc.psum_tensor(f"pX{u}", [P, 512], F32)) for u in range(2)]
        pY = [ctx.enter_context(nc.psum_tensor(f"pY{u}", [P, 512], F32)) for u in range(2)]
        ps_low = pX[1][:, 0:P]
        ps_hc = pA[0][:, 512:512 + CB * D].rearrange("p (c d) -> p c d", c=CB)
        ps_lT = pA[1][0:R1, 0:CB * P]
        ps_g = pX[0][0:R1, 0:R1]
        ps_v = pX[0][0:R1, P:P + DL]
        ps_b = pY[0][0:R1, 0:DL]
        ps_o = pY[1][:, 0:CB * DL].rearrange("p (c d) -> p c d", c=CB)
        ps_pr = pA[1][:, 0:D]
        ps_mean = pA[1][0:D // 2, 512:512 + RANK]
        ps_w = [ps[0:D // 2, 0:2 * D].rearrange("p (b n) -> p b n", b=2) for ps in (pX[0], pY[0], pY[1])]
        ps_m2 = pY[1][0:RANK, 0:D]
        ps_vkqc = pY[0][0:D // 2, 0:6 * RANK].rearrange("p (m a r) -> p m a r", m=3, a=2)
        ps_gmean = pA[1][0:D // 2, 512 + P:512 + P + 4 * C]
        ps_M2g, ps_PTg = pA[1][0:R1, 512 + 2 * P:512 + 2 * P + 4 * C], pA[1][:, 512 + 3 * P:512 + 3 * P + 4 * C]
        ps_m1 = pY[1][0:R1, 0:R1]
        ps_2m, ps_2r = pY[0][:, D:D + EX], pY[0][0:DR, D + EX:D + 2 * EX]
        ps_2p = pY[1][0:EX, 0:D]
        ps_rank = pX[0][:, 0:NT * EX].rearrange("p (i e) -> p i e", e=EX)
        ps_tot = pX[1][:, 0:NT * EX].rearrange("p (e i) -> p e i", e=EX)
        ps_inv = pY[0][:, 0:ST]
        ps_expert_row = pY[1][0:1, 0:P]
        ps_experts = pY[1][0:1, 0:STP]

        ps_y = [[pY[c][:, 0:D] for c in range(CB)]] + [[pA[u][:, 512 * c:512 * c + D] for c in range(CB)] for u in range(2)]

        ids_in = sem("ids_in")
        gathered = [sem(f"gathered{b}") for b in range(B)]
        proj_in, vkq_in, gate_in, tail_in, b2_in, b2p_in = (sem(n) for n in (
            "proj_in", "vkq_in", "gate_in", "tail_in", "b2_in", "b2p_in"))
        consts, idle_set = sem("consts"), sem("idle_set")
        dve_done = sem("dve_done")
        masks = sem("masks")
        zeros, PT_done = sem("zeros"), sem("PT_done")
        projT_mm, projT_ev, mean_mm, PcT_done, Pc_done = (sem(n) for n in (
            "projT_mm", "projT_ev", "mean_mm", "PcT_done", "Pc_done"))
        vkqT_mm, vkqT_ev, M2_mm, M2_ev, kq_mm, kq_ev, M1_mm, M1_ev, kq_bias = (sem(n) for n in (
            "vkqT_mm", "vkqT_ev", "M2_mm", "M2_ev", "kq_mm", "kq_ev", "M1_mm", "M1_ev", "kq_bias"))
        b2T_mm, b2T_ev, b2p_mm, b2p_ev = (sem(n) for n in ("b2T_mm", "b2T_ev", "b2p_mm", "b2p_ev"))
        low_mm, low_ev = sem("low_mm"), sem("low_ev")
        h_mm, h_read, l_done = sem("h_mm"), sem("h_read"), sem("l_done")
        var12, sd12 = sem("var12"), sem("sd12")
        lT_mm, lT_ev = sem("lT_mm"), sem("lT_ev")
        gram_mm, gram_ev = sem("gram_mm"), sem("gram_ev")
        gv_mm, gv_ev = sem("gv_mm"), sem("gv_ev")
        bb_mm, bb_ev = sem("bb_mm"), sem("bb_ev")
        att_mm, h2_ev, x2_done = sem("att_mm"), sem("h2_ev"), sem("x2_done")
        x2_out = sem("x2_out")
        norm2 = sem("norm2")
        gate_b_in, gmean_mm, gates_done, gates_mm = (sem(n) for n in ("gate_b_in", "gmean_mm", "gates_done", "gates_mm"))
        lg_ready, lg_exp = sem("lg_ready"), sem("lg_exp")
        picked, counted = sem("picked"), sem("counted")
        hot, inv_mm, routed, pool_done, slots_known, ends_known, experts_known, proj_twice = (sem(n) for n in (
            "hot", "inv_mm", "routed", "pool_done", "slots_known", "ends_known", "experts_known", "proj_twice"))
        resid = sem("resid")
        token_copied, dest_copied, pool_passed = sem("token_copied"), sem("dest_copied"), sem("pool_passed")
        tok_in = [sem(f"tok_in{u}") for u in range(SLOTS)]
        w_in = [sem(f"w_in{u}") for u in range(SLOTS)]
        sent = [sem(f"sent{u}") for u in range(SLOTS)]
        xs_mm, xs_ev, up_mm, gelu_done, down_mm, y_ev = (sem(n) for n in (
            "xs_mm", "xs_ev", "up_mm", "gelu_done", "down_mm", "y_ev"))
        moe_done = sem("moe_done")
        ys_in = [sem(f"ys_in{b}") for b in range(B)]
        y1w, mix_done, mixT_mm, mixT_ev, proj_mm, fin_done, fin_out = (sem(n) for n in (
            "y1w", "mix_done", "mixT_mm", "mixT_ev", "proj_mm", "fin_done", "fin_out"))
        var3, sd3, root_step, norm3, z_done, gam_done = (sem(n) for n in (
            "var3", "sd3", "root_step", "norm3", "z_done", "gam_done"))

        W1_e = W1.rearrange("g e d h -> (g e) d h")
        b1_e = b1.rearrange("g e h -> (g e) h")
        W2_e = W2.rearrange("g e (p j) d -> (g e) p (j d)", j=HC)
        x_store = x_rows.rearrange("(p i) d -> p i d", i=NT)
        y_load = y_rows[0:K * TOKENS, :].rearrange("(k p i) d -> k p i d", k=K, i=NT)
        out_b = out.rearrange("b (p c) d -> b p c d", c=CB)

        STEPS = B + 3

        def stage(s, off):
            return 0 <= s - off < B

        def norms(s):
            return slice(0, 2 if stage(s, 3) else 1) if s < B else slice(3, 3 + LATE)

        def tiles_in_use(eng):
            eng.wait_ge(experts_known, 1)
            return eng.value_load(tiles_used[0:1, 0:1], min_val=FULL * SLOTS, max_val=ST)

        block = ctx.enter_context(nc.Block())

        @block.sync
        def _(sp):
            with nc.allow_non_contiguous_dma(reason="small weights and ids"):
                sp.dma_start(ids[:, :].rearrange("p (b c) -> p b c", c=CB),
                             x.rearrange("b (p c) -> p b c", c=CB)).then_inc(ids_in, 16)
                sp.dma_start(proj_s[:, :, 0, :], proj.rearrange("(p a) r -> p a r", a=2)).then_inc(proj_in, 16)
                for n, (w, b) in enumerate(((Wv, bv), (Wk, bk), (Wq, bq))):
                    sp.dma_start(vkq[:, n, :, 0:D], w.rearrange("(p a) d -> p a d", a=2)).then_inc(vkq_in, 16)
                for n, b in enumerate((bv, bk, bq)):
                    sp.dma_start(vkq[:, n, :, D:D1], b.rearrange("(p a o) -> p a o", a=2, o=1)).then_inc(vkq_in, 16)
                sp.wait_ge(zeros, 1)
                sp.dma_start(M2[RANK:R1, 0:D], bv.rearrange("(a d) -> a d", a=1)).then_inc(vkq_in, 16)
                we = We.rearrange("g d e -> d g e")
                sp.dma_start(gates[:, :, 0, :], Wg.rearrange("(p a) e -> p a e", a=2)).then_inc(gate_in, 16)
                for a in range(2):
                    sp.dma_start(gates[:, a, 1:C, :], we.rearrange("(p a) g e -> a p g e", a=2)[a]).then_inc(gate_in, 16)
                sp.dma_start(gate_b[:, 0, :], bg.partition_broadcast(P)).then_inc(gate_b_in, 16)
                sp.dma_start(gate_b[:, 1:C, :], be.partition_broadcast(P)).then_inc(gate_b_in, 16)
                sp.dma_start(b2_s[:, :], b2.rearrange("g e d -> (g e) d")).then_inc(b2_in, 16)
                sp.dma_start(Wp_m[:, :], Wp[0:P, :]).then_inc(b2_in, 16)
                sp.dma_start(Wp_r[0:DR, :], Wp[P:D, :]).then_inc(b2_in, 16)
                sp.dma_start(Wp_r[DR + EX:DR + EX + 1, :], bp.rearrange("(a d) -> a d", a=1)).then_inc(tail_in, 16)
                sp.dma_start(gam[:, :], gamma.partition_broadcast(P)).then_inc(tail_in, 16)
                sp.dma_start(bet[:, :], beta.partition_broadcast(P)).then_inc(tail_in, 16)
            for b in range(B):
                sp.wait_ge(x2_done, b + 1)
                sp.dma_start(x_store[:, CB * b:CB * b + CB, :], x2[:, CB * b:CB * b + CB, :]).then_inc(x2_out, 16)

            sp.wait_ge(b2p_ev, 1)
            sp.dma_start(Wp_r[DR:DR + EX, :], b2p[:, :]).then_inc(b2p_in, 16)

            sp.wait_ge(experts_known, 1)
            sp.wait_ge(runs_known, 1)

            def load(t, u):
                e = sp.value_load(expert[0:1, bass.ds(t, 1)], min_val=0, max_val=EX - 1)
                sp.dma_start(W1_m[u][:, :], W1_e[bass.ds(e, 1), 0:P, :].rearrange("a d h -> (a d) h")).then_inc(w_in[u], 16)
                sp.dma_start(W1_r[u][0:DR, :], W1_e[bass.ds(e, 1), P:D, :].rearrange("a d h -> (a d) h")).then_inc(w_in[u], 16)
                sp.dma_start(W1_r[u][DR:DR + 1, :], b1_e[bass.ds(e, 1), :]).then_inc(w_in[u], 16)
                sp.dma_start(W2_s[u][:, :, :].rearrange("p j d -> p (j d)"), W2_e[bass.ds(e, 1)].rearrange("a p n -> (a p) n")).then_inc(w_in[u], 16)

            for t in range(SLOTS):
                if t == SLOTS - 2:
                    sp.wait_ge(pool_passed, 2)
                load(t, t)

            def renew(t, v):
                new = sp.value_load(expert[0:1, bass.ds(t, 1)], min_val=0, max_val=EX - 1)
                old = sp.value_load(expert[0:1, bass.ds(t - SLOTS, 1)], min_val=0, max_val=EX - 1)
                with sp.If(new != old):
                    load(t, v)
                with sp.Else():
                    sp.sem_inc(w_in[v], 64)

            def body(t, u):
                sp.wait_ge(down_mm, t)
                renew(t + SLOTS - 1, (u + SLOTS - 1) % SLOTS)

            for u in range(1, SLOTS):
                body(u, u)
            with sp.Fori(1, FULL) as i:
                for u in range(SLOTS):
                    body(i * SLOTS + u, u)
            used = tiles_in_use(sp)
            with sp.Fori(FULL, ROUNDS) as i:
                for u in range(SLOTS):
                    v = (u + SLOTS - 1) % SLOTS
                    with sp.If(used > i * SLOTS + u + SLOTS - 1):
                        sp.wait_ge(down_mm, i * SLOTS + u)
                        renew(i * SLOTS + u + SLOTS - 1, v)

            loaded = sp.value_load(steps_loaded[0:1, 0:1], min_val=AHEAD, max_val=ST)
            for u in range(SLOTS):
                sp.wait_ge(w_in[u], (loaded + (SLOTS - 1 - u)) // SLOTS * 64)
            sp.wait_ge(moe_done, 1)
            for b in range(B):
                sp.dma_start(ys[:, :, CB * b:CB * b + CB, :].rearrange("p k i d -> p k (i d)"),
                             y_load[:, :, CB * b:CB * b + CB, :].rearrange("k p i d -> p k (i d)")).then_inc(ys_in[b], 16)
            for b in range(B):
                sp.wait_ge(fin_done, b + 1)
                sp.dma_start(out_b[b], fin[:, CB * b:CB * b + CB, :]).then_inc(fin_out, 16)
            sp.wait_ge(fin_out, 16 * B)

        @block.gpsimd
        def _(pool):
            iota = dict(allow_small_or_imprecise_dtypes=True)
            pool.iota(diff[:, :], [[1, P]], base=0, channel_multiplier=-1, **iota).then_inc(consts, 1)
            pool.iota(step_i[:, 0:1], [[0, 1]], base=0, channel_multiplier=1).then_inc(consts, 1)
            pool.wait_ge(ids_in, 16)
            for i in range(NT):
                pool.indirect_dma_start(emb[:, i, :], None, table, bass.IndirectOffsetOnAxis(
                    ap=ids[:, i:i + 1].bitcast(U32), axis=0)).then_inc(gathered[i // CB], 16)
            pool.iota(lane[:, :], [[1, P]], base=0, channel_multiplier=0, **iota).then_inc(consts, 1)
            pool.iota(rank4[:, :], [[-1, G]], base=G, channel_multiplier=0, **iota).then_inc(consts, 1)
            pool.iota(fill[:, :], [[-1, SLOTS - 1]], base=SLOTS - 1, channel_multiplier=0, **iota).then_inc(consts, 1)
            pool.iota(row_id[:, 0, :], [[1, NT]], base=1, channel_multiplier=NT, **iota).then_inc(consts, 1)
            pool.iota(row_id[:, 1, :], [[-1, NT]], base=-1, channel_multiplier=-NT, **iota).then_inc(consts, 1)
            pool.iota(dump[:, :, :], [[0, ROUNDS], [P, SLOTS]], base=K * TOKENS, channel_multiplier=1, **iota).then_inc(consts, 1)
            pool.memset(token_of[:, ST:STP], 0).then_inc(consts, 1)
            for i in range(NT):
                if i % CB == 0:
                    pool.wait_ge(norm2, i // CB + 1)
                ins = pool.tensor_scalar(x2[:, i, 0:D], h2[:, i, :], mu2[:, i:i + 1], rs2[:, i:i + 1], ALU.subtract, ALU.mult)
                if i % CB == CB - 1:
                    ins.then_inc(x2_done, 1)

            pool.wait_ge(ends_known, 1)
            pool.wait_ge(masks, 3)
            pool.wait_ge(runs_known, 1)
            steps = [0]

            def linked(ins):
                steps[0] += 1
                ins.then_inc(pool_done, 1)
                pool.wait_ge(pool_done, steps[0])

            linked(pool.tensor_tensor(skipped[:, :], later[:, :], run[:, :], ALU.mult))
            into = step_f[:, 0:1]
            for k in range(SLOTS - 1):
                linked(pool.tensor_tensor(tile_of[:, :], into, skipped[:, k:k + 1], ALU.add))
                into = tile_of[:, :]
            linked(pool.tensor_tensor(past[:, :], tile_of[:, :].to_broadcast([P, EX]), end_e[:, :], ALU.subtract))
            linked(pool.tensor_scalar(past[:, :], past[:, :], 0.0, None, ALU.is_ge))
            width = EX // 2
            while width:
                into = past[:, 0:width] if width > 1 else expert_f[:, :]
                linked(pool.tensor_tensor(into, past[:, 0:width], past[:, width:2 * width], ALU.add))
                width //= 2
            pool.tensor_scalar(expert_f[:, :], expert_f[:, :], float(EX - 1), None, ALU.min).then_inc(experts_counted, 1)
            pool.tensor_copy(rows_h[:, :], row_id[:, :, :].rearrange("p k i -> p (k i)")).then_inc(rows_done, 1)
            pool.wait_ge(rows_done, 1)
            for q in range(K * NT // GROUP):
                ms = slice(q * GROUP, (q + 1) * GROUP)
                pool.wait_ge(hot_own, q + 1)
                pool.tensor_tensor(hot_tile[:, ms, :], hot_tile[:, ms, :],
                                   rows_h[:, ms].unsqueeze(2).to_broadcast([P, GROUP, ST]), ALU.mult).then_inc(hot_row, 1)

            pool.wait_ge(tokens_known, 1)
            pool.wait_ge(x2_out, 16 * B)

            def gather(t, u):
                pool.tensor_copy(token_i[u][:, :], token_of[:, bass.ds(t, 1)]).then_inc(token_copied, 1)
                pool.wait_ge(token_copied, t + 1)
                pool.sem_inc(pool_passed, 1)
                pool.indirect_dma_start(xg[u][:, :], None, x_rows, bass.IndirectOffsetOnAxis(
                    ap=token_i[u][:, :].bitcast(U32), axis=0)).then_inc(tok_in[u], 16)

            for t in range(SLOTS):
                gather(t, t)
            pool.wait_ge(tail_in, 48)
            pool.wait_ge(x2_done, B)
            pool.tensor_tensor(h2[:, :, :], h2[:, :, :], bet[:, :].unsqueeze(1).to_broadcast([P, NT, D]),
                               ALU.add).then_inc(resid, 1)
            pool.wait_ge(xs_mm, 1)
            gather(SLOTS, 0)
            pool.wait_ge(routed, 1)

            def body(t, u, i):
                pool.wait_ge(xs_mm, t + 2)
                gather(t + SLOTS + 1, (u + 1) % SLOTS)
                at_least(pool, sent[u], 16 * i)
                pool.tensor_copy(dest_i[u][:, :], dest_of[:, bass.ds(t, 1)]).then_inc(dest_copied, 1)
                pool.wait_ge(dest_copied, t + 1)
                pool.wait_ge(y_ev, t + 1)
                pool.sem_inc(pool_passed, 1)
                pool.indirect_dma_start(y_rows, bass.IndirectOffsetOnAxis(
                    ap=dest_i[u][:, :].bitcast(U32), axis=0), yo[u][:, :], None).then_inc(sent[u], 16)

            for u in range(SLOTS):
                body(u, u, 0)
            with pool.Fori(1, FULL) as i:
                for u in range(SLOTS):
                    body(i * SLOTS + u, u, i)
            used = tiles_in_use(pool)
            with pool.Fori(FULL, ROUNDS) as i:
                for u in range(SLOTS):
                    with pool.If(used > i * SLOTS + u):
                        body(i * SLOTS + u, u, i)
            for u in range(SLOTS):
                pool.wait_ge(sent[u], (used + (SLOTS - 1 - u)) // SLOTS * 16)
                pool.wait_ge(tok_in[u], (used + (2 * SLOTS - u)) // SLOTS * 16)
            pool.sem_inc(moe_done, 1)
            for b in range(B - 1):
                tiles = slice(CB * b, CB * b + CB)
                pool.wait_ge(z_done, CB * b + CB)
                pool.tensor_tensor(fin[:, tiles, :], fin[:, tiles, :], gam[:, :].unsqueeze(1).to_broadcast([P, CB, D]),
                                   ALU.mult).then_inc(gam_done, 1)
                pool.wait_ge(gam_done, b + 1)
                pool.tensor_tensor(fin[:, tiles, :], fin[:, tiles, :], h2[:, tiles, :], ALU.add).then_inc(fin_done, 1)

        @block.scalar
        def _(act):
            def copy(dst, src, s=None):
                ins = nc.scalar.activation(dst, src, ACT.Copy)
                if s is not None:
                    ins.then_inc(s, 1)

            loads = [0]

            def load_table(function):
                loads[0] += 1
                nc.scalar.activation(idle[:, loads[0]:loads[0] + 1], idle[:, 0:1], function)

            def exponentials(lo, hi):
                act.wait_ge(lg_ready, 1 if lo == 0 else 2)
                nc.scalar.activation(lg[:, C * lo:C * hi, :], lx[:, C * lo:C * hi, :], ACT.Exp).then_inc(lg_exp, 1)

            act.wait_ge(projT_mm, 1)
            act.wait_ge(zeros, 1)
            copy(projT[:, :].rearrange("q (p a) -> q a p", a=2), ps_pr.rearrange("q (a p) -> q a p", a=2), projT_ev)
            act.wait_ge(projT_ev, 1)
            for c in range(CB):
                rows = slice(c * RANK, (c + 1) * RANK)
                copy(PT[rows, c, 0:D], projT[rows, :], PT_done)
            act.wait_ge(idle_set, 1)
            load_table(ACT.Sqrt)

            def low_turned(b):
                act.wait_ge(low_mm, b + 1)
                copy(lowT[:, b, :], ps_low, low_ev)

            def roots(s, count):
                act.wait_ge(var12, count)
                nc.scalar.activation(sd[:, norms(s), :], ve[:, norms(s), :], ACT.Sqrt).then_inc(sd12, 1)

            low_turned(0)
            for s in range(STEPS):
                if s == 0:
                    for m in range(3):
                        act.wait_ge(vkqT_mm, m + 1)
                        copy(vkqT[:, m, :, :], ps_w[m], vkqT_ev)
                if stage(s, 2):
                    b = s - 2
                    act.wait_ge(gram_mm, b + 1)
                    at_least(act, gv_mm, b - 1)
                    copy(gram[0:R1, b % 2, :], ps_g, gram_ev)
                    act.wait_ge(lT_mm, b + 1)
                    at_least(act, att_mm, b - 1)
                    copy(lT[0:R1, b % 2, :], ps_lT, lT_ev)
                if stage(s, 0) and s > 0:
                    low_turned(s)
                if s == B + 1:
                    exponentials(0, EARLY)
                if stage(s, 3):
                    b = s - 3
                    act.wait_ge(att_mm, b + 1)
                    copy(h2[:, CB * b:CB * b + CB, :], ps_o[:, :, 0:D])
                    copy(raw[:, CB * b:CB * b + CB, :], ps_o[:, :, D:DL], h2_ev)
                if stage(s, 2):
                    b = s - 2
                    act.wait_ge(gv_mm, b + 1)
                    at_least(act, bb_mm, b - 1)
                    copy(gv[0:R1, b % 2, :], ps_v, gv_ev)
                    act.wait_ge(bb_mm, b + 1)
                    at_least(act, att_mm, b - 1)
                    copy(bb[0:R1, b % 2, :], ps_b, bb_ev)
                if s < B:
                    roots(s, s + 1)
                if s == 1:
                    act.wait_ge(M2_mm, 1)
                    copy(M2[0:RANK, 0:D].rearrange("q (p a) -> q a p", a=2), ps_m2.rearrange("q (a p) -> q a p", a=2), M2_ev)
                    act.wait_ge(kq_mm, 1)
                    copy(vkqc[:, :, :, 0:RANK], ps_vkqc, kq_ev)
                    act.wait_ge(M1_mm, 1)
                    nc.scalar.activation(M1T[0:R1, :], ps_m1, ACT.Copy, scale=float(D) ** -0.5).then_inc(M1_ev, 1)
                    act.wait_ge(gates_mm, 1)
                    copy(M2[0:R1, D:DL], ps_M2g, M2_ev)
                    for c in range(CB):
                        rows = slice(c * RANK, (c + 1) * RANK)
                        copy(PT[rows, c, D:DL], ps_PTg[rows, :], PT_done)
                if s == B:
                    load_table(ACT.Exp)
                if s == B + 1:
                    load_table(ACT.Sqrt)
            roots(B + 2, B + 1)
            load_table(ACT.Exp)

            act.wait_ge(b2T_mm, 1)
            copy(b2T_m[:, :], ps_2m)
            copy(b2T_r[:, :], ps_2r, b2T_ev)
            exponentials(EARLY, NT)
            load_table(ACT.Gelu)
            act.wait_ge(b2p_mm, 1)
            copy(b2p[:, :], ps_2p, b2p_ev)
            act.wait_ge(experts_mm, 1)
            copy(expert[:, :], ps_experts)
            copy(tiles_used[:, :], end_e[0:1, EX - 1:EX], experts_known)

            def body(t, u):
                v = u % 2
                act.wait_ge(up_mm, t + 1)
                at_least(act, down_mm, t - 1)
                nc.scalar.activation(hT[v][:, :], pA[v][:, 0:H], ACT.Gelu).then_inc(gelu_done, 1)

            for u in range(SLOTS):
                body(u, u)
            with act.Fori(1, FULL) as i:
                for u in range(SLOTS):
                    body(i * SLOTS + u, u)
            used = tiles_in_use(act)
            with act.Fori(FULL, ROUNDS) as i:
                for u in range(SLOTS):
                    with act.If(used > i * SLOTS + u):
                        body(i * SLOTS + u, u)

            load_table(ACT.Sqrt)
            def scaled(i):
                act.wait_ge(ys_in[i // CB], 16)
                nc.scalar.activation(ys[:, 0, i, :], ys[:, 0, i, :], ACT.Copy, scale=wk[:, 0, i:i + 1]).then_inc(y1w, 1)

            def turned_mix(j):
                act.wait_ge(mixT_mm, j + 1)
                at_least(act, proj_mm, j - 1)
                copy(mixT_m[:, j % 2, :], pX[j % 2][:, 0:P])
                copy(mixT_r[:, j % 2, :], pX[j % 2][0:DR + EX + 1, P:2 * P], mixT_ev)

            for i in range(CB):
                scaled(i)
            for i in range(CB):
                scaled(CB + i)
                turned_mix(i)
            for i in range(CB):
                scaled(2 * CB + i)
                turned_mix(CB + i)
            for b in range(B):
                act.wait_ge(var3, b + 1)
                nc.scalar.activation(sd[:, 2, :], ve[:, 2, :], ACT.Sqrt).then_inc(sd3, 1)
                if b + 3 < B:
                    for c in range(CB):
                        scaled(CB * (b + 3) + c)
                if b + 2 < B:
                    turned_mix(CB * (b + 2))
                act.wait_ge(norm3, b + 1)
                for c in range(CB):
                    nc.scalar.activation(fin[:, CB * b + c, :], ps_y[b % 3][c], ACT.Identity, bias=nm[:, c:c + 1],
                                         scale=rs[:, 2, c:c + 1]).then_inc(z_done, 1)
                if b + 2 < B:
                    turned_mix(CB * (b + 2) + 1)

        @block.vector
        def _(dve):
            made = [0]

            def link(ins):
                made[0] += 1
                ins.then_inc(dve_done, 1)
                dve.wait_ge(dve_done, made[0])

            for buffer in (PcT, PT, M1T, M2, lT, gram, gv, bb):
                ins = nc.vector.memset(buffer[:], 0.0)
            ins.then_inc(zeros, 1)
            nc.vector.memset(ones[:, :], 1.0)
            nc.vector.memset(carry[:, :, :], 1.0)
            nc.vector.memset(unit[:, :], 1.0)
            nc.vector.memset(idle[:, :], 1.0).then_inc(idle_set, 1)
            nc.vector.memset(x2[:, :, D:ROW], 1.0)
            nc.vector.memset(mixw[:, :, D + EX:D + EX + 1], 1.0)
            nc.vector.memset(mean_w[:, :], 1.0 / D)
            link(nc.vector.memset(lh[:, :, :, RANK:R1], 1.0))
            nc.vector.memset(carry[:, :, 0:1], 0.0)
            dve.wait_ge(consts, 1)
            nc.vector.tensor_scalar(ident[:, :], diff[:, :], 0.0, None, ALU.is_equal).then_inc(masks, 1)
            dve.wait_ge(proj_in, 16)
            nc.vector.tensor_copy(proj_s[:, :, 1, :], proj_s[:, :, 0, :]).then_inc(proj_twice, 1)
            nc.vector.tensor_scalar(before[:, :], diff[:, :], 0.0, -1.0, ALU.is_gt, ALU.add).then_inc(masks, 1)
            dve.wait_ge(consts, 2)
            nc.vector.tensor_scalar(step_i[:, 1:2], step_i[:, 0:1], 2, None, ALU.arith_shift_right)
            link(nc.vector.tensor_scalar(step_i[:, 2:3], step_i[:, 0:1], SLOTS - 1, None, ALU.bitwise_and))
            link(nc.vector.tensor_copy(step_f[:, :], step_i[:, 1:3]))
            for k in range(1, SLOTS):
                ins = nc.vector.tensor_scalar(later[:, k - 1:k], step_f[:, 1:2], float(k), None, ALU.is_ge)
            ins.then_inc(masks, 1)
            dve.wait_ge(projT_ev, 1)
            link(nc.vector.bn_stats(pmean[:, 0:6], projT[:, :]))
            link(nc.vector.bn_aggr(pmean[:, 6:8], pmean[:, 0:6]))
            for c in range(CB):
                rows = slice(c * RANK, (c + 1) * RANK)
                ins = nc.vector.tensor_scalar(PcT[rows, c, :], projT[rows, :], pmean[rows, 6:7], None, ALU.subtract)
            ins.then_inc(PcT_done, 1)
            dve.wait_ge(mean_mm, 1)
            nc.vector.tensor_tensor(Pc[:, :, :], proj_s[:, :, 0, :], ps_mean.unsqueeze(1).to_broadcast([D // 2, 2, RANK]),
                                    ALU.subtract).then_inc(Pc_done, 1)
            dve.wait_ge(vkq_in, 112)
            nc.vector.tensor_copy(vkqc[:, :, :, RANK:R1], vkq[:, :, :, D:D1]).then_inc(kq_bias, 1)

            def root_input(n, ready):
                nc.vector.tensor_scalar(ve[:, n, :], mv[:, n, :, 1], EPS, 0.25, ALU.add, ALU.mult).then_inc(ready, 1)

            def newton(n):
                link(nc.vector.tensor_tensor(tn[:, n, :], rs[:, n, :], ve[:, n, :], ALU.mult))
                return nc.vector.tensor_tensor(tn[:, n, :], tn[:, n, :], sd[:, n, :], ALU.add)

            def inverse_root(n, root, count):
                dve.wait_ge(root, count)
                link(nc.vector.reciprocal(rs[:, n, :], sd[:, n, :]))
                link(newton(n))
                link(nc.vector.reciprocal(rs[:, n, :], tn[:, n, :]))

            V = nc.vector

            def exponents(lo, hi, n):
                rows = slice(C * lo, C * hi)
                N = C * (hi - lo)
                lg_v = lg[:, rows, :].rearrange("p (i c) e -> p i (c e)", c=C)
                link(V.tensor_tensor(lg_v, raw[:, lo:hi, :], rs2[:, lo:hi].unsqueeze(2).to_broadcast([P, hi - lo, 4 * C]), ALU.mult))
                link(V.tensor_tensor(lg_v, lg_v, gate_b[:, :, :].rearrange("p c e -> p (c e)").unsqueeze(1).to_broadcast(
                    [P, hi - lo, 4 * C]), ALU.add))
                link(V.tensor_reduce(r4[:, rows], lg[:, rows, :], AX.X, ALU.max))
                V.tensor_tensor(lx[:, rows, :], lg[:, rows, :], r4[:, rows].unsqueeze(2).to_broadcast([P, N, 4]),
                                ALU.subtract).then_inc(lg_ready, 1)

            def probabilities(lo, hi, n):
                rows = slice(C * lo, C * hi)
                N = C * (hi - lo)
                dve.wait_ge(lg_exp, n)
                link(V.tensor_reduce(r4[:, rows], lg[:, rows, :], AX.X, ALU.add))
                link(V.reciprocal(r4[:, rows], r4[:, rows]))
                link(V.tensor_tensor(pr_v[:, rows, :], lg[:, rows, :], r4[:, rows].unsqueeze(2).to_broadcast([P, N, 4]),
                                     ALU.mult))

            def top(chosen, best, prob, n, keys, kbest):
                link(V.tensor_reduce(best, prob, AX.X, ALU.max))
                link(V.tensor_tensor(chosen, prob, best.unsqueeze(2).to_broadcast([P, n, 4]), ALU.is_equal))
                link(V.tensor_tensor(keys, chosen, rank4[:, :].unsqueeze(1).to_broadcast([P, n, 4]), ALU.mult))
                link(V.tensor_reduce(kbest, keys, AX.X, ALU.max))
                return V.tensor_tensor(chosen, keys, kbest.unsqueeze(2).to_broadcast([P, n, 4]), ALU.is_equal)

            def pick(lo, hi):
                rows, tiles, n = slice(C * lo, C * hi), slice(lo, hi), hi - lo
                link(top(first_v[:, rows, :], pmax_v[:, rows], pr_v[:, rows, :], C * n, key[:, rows, :], kmax[:, rows]))
                link(V.scalar_tensor_tensor(out=pg2[:, tiles, :], in0=first[:, tiles, 0, :], scalar=-4.0,
                                            in1=pr[:, tiles, 0, :], op0=ALU.mult, op1=ALU.add))
                link(top(second[:, tiles, :], gmax2[:, tiles], pg2[:, tiles, :], n, key[:, 0:n, :], kmax[:, 0:n]))
                for k, group in enumerate((first[:, tiles, 0, :], second[:, tiles, :])):
                    ins = V.tensor_tensor(sel[:, k, tiles, :].rearrange("p i (g e) -> p i g e", g=G),
                                          group.unsqueeze(3).to_broadcast([P, n, G, E]), first[:, tiles, 1:C, :], ALU.mult)
                link(ins)
                return V.tensor_tensor(both[:, tiles, :], sel[:, 0, tiles, :], sel[:, 1, tiles, :], ALU.add)

            for s in range(STEPS):
                if stage(s, 3):
                    b = s - 3
                    dve.wait_ge(h2_ev, b + 1)
                    for c in range(CB):
                        ins = V.bn_stats(stats[:, 1, c, :], h2[:, CB * b + c, :])
                if stage(s, 0):
                    dve.wait_ge(h_mm, s + 1)
                    for c in range(CB):
                        ins = V.bn_stats(stats[:, 0, c, :], ps_hc[:, c, :])
                    ins.then_inc(h_read, 1)
                    dve.wait_ge(h_read, s + 1)
                else:
                    link(ins)
                if s >= B:
                    for c in range(CB):
                        ins = V.bn_aggr(mv[:, 3 + s - B, c, :], stats[:, 1, c, :])
                    link(ins)
                    if s == B:
                        dve.wait_ge(gate_b_in, 32)
                        dve.wait_ge(consts, 9)
                        exponents(0, EARLY, 1)
                        probabilities(0, EARLY, 1)
                        link(pick(0, EARLY))
                    continue
                ns = norms(s)
                for n in range(ns.start, ns.stop):
                    for c in range(CB):
                        ins = V.bn_aggr(mv[:, n, c, :], stats[:, n, c, :])
                link(ins)
                root_input(ns, var12)
                inverse_root(ns, sd12, s + 1)
                b = s
                at_least(dve, lT_mm, b - 1)
                for c in range(CB):
                    ins = V.tensor_scalar(lh[:, b % 2, c, 0:RANK], emb[:, CB * b + c, :], rs[:, 0, c:c + 1], None, ALU.mult)
                ins.then_inc(l_done, 1)
                if stage(s, 3):
                    tiles = slice(CB * (s - 3), CB * (s - 2))
                    V.tensor_copy(mu2[:, tiles], mv[:, 1, :, 0])
                    link(V.tensor_copy(rs2[:, tiles], rs[:, 1, :]))
                    dve.sem_inc(norm2, 1)
                if s == 0:
                    dve.wait_ge(gmean_mm, 1)
                    V.tensor_tensor(gates_c[:, :, :], gates[:, :, :, :].rearrange("p a c e -> p a (c e)"),
                                    ps_gmean.unsqueeze(1).to_broadcast([D // 2, 2, 4 * C]), ALU.subtract).then_inc(gates_done, 1)

            ns = norms(B + 2)
            root_input(ns, var12)
            inverse_root(ns, sd12, B + 1)
            V.tensor_copy(mu2[:, EARLY:NT].rearrange("p (b c) -> p b c", c=CB), mv[:, ns, :, 0])
            link(V.tensor_copy(rs2[:, EARLY:NT].rearrange("p (b c) -> p b c", c=CB), rs[:, ns, :]))
            dve.sem_inc(norm2, LATE)
            exponents(EARLY, NT, 2)
            probabilities(EARLY, NT, 2)
            pick(EARLY, NT).then_inc(picked, 1)
            dve.wait_ge(counted, 1)
            link(V.tensor_tensor_scan(upto[:, :, :].rearrange("p e i -> p (e i)"),
                                      carry[:, :, :].rearrange("p e i -> p (e i)"),
                                      ps_tot.rearrange("p e i -> p (e i)"), 0.0, ALU.mult, ALU.add))
            link(V.tensor_scalar(count_i[:, 0, :], upto[:, :, NT - 1], float(P - 1), None, ALU.add))
            link(V.tensor_scalar(count_i[:, 1, :], count_i[:, 0, :], 7, None, ALU.arith_shift_right))
            link(V.tensor_copy(tiles_e[:, :], count_i[:, 1, :]))
            link(V.tensor_tensor_scan(end_e[:, :], unit[:, :], tiles_e[:, :], 0.0, ALU.mult, ALU.add))
            link(V.tensor_tensor(base_e[:, :], end_e[:, :], tiles_e[:, :], ALU.subtract))
            V.tensor_scalar(base_e[:, :], base_e[:, :], float(P), None, ALU.mult).then_inc(ends_known, 1)
            dve.wait_ge(ends_known, 1)
            V.tensor_tensor(run_i[:, 0, :], end_e[:, EX - 1:EX].to_broadcast([P, SLOTS - 1]), fill[:, :], ALU.add)
            link(V.tensor_tensor(upto[:, :, :], upto[:, :, :], base_e[:, :].unsqueeze(2).to_broadcast([P, EX, NT]), ALU.add))
            V.tensor_scalar(run_i[:, 1, :], run_i[:, 0, :], 2, None, ALU.arith_shift_right)
            link(V.tensor_tensor(place[:, :, :], ps_rank, upto[:, :, :].rearrange("p e i -> p i e"), ALU.add))
            V.tensor_scalar(steps_loaded[:, :], end_e[0:1, EX - 1:EX], float(AHEAD), None, ALU.max)
            V.tensor_copy(run[:, :], run_i[:, 1, :]).then_inc(runs_known, 1)
            link(V.tensor_tensor(placed[:, :, :, :], sel[:, :, :, :],
                                 place[:, :, :].unsqueeze(1).to_broadcast([P, K, NT, EX]), ALU.mult))
            V.tensor_tensor_scan(run_end[:, :], unit[:, 0:SLOTS - 1], run[:, :], 0.0, ALU.mult, ALU.add)
            V.tensor_scalar(run_step[:, :], run[:, :], -float(SLOTS), 1.0, ALU.mult, ALU.add)
            link(V.tensor_reduce(slot_f[:, :], placed[:, :, :, :].rearrange("p k i e -> p (k i) e"), AX.X, ALU.add))
            link(V.tensor_copy(slot_i[:, :], slot_f[:, :]))
            V.tensor_scalar(slot_t[:, 0, :], slot_i[:, :], 7, None, ALU.arith_shift_right)
            link(V.tensor_scalar(slot_t[:, 1, :], slot_i[:, :], P - 1, None, ALU.bitwise_and))
            V.tensor_copy(slot_p[:, :, :], slot_t[:, :, :]).then_inc(slots_known, 1)
            dve.wait_ge(slots_known, 1)
            pairs = [P, SLOTS - 1, K * NT]

            def one_hots(hots, numbers, lo, hi):
                shape = [P, hi - lo, hots.shape[2]]
                return V.tensor_tensor(hots[:, lo:hi, :], lane[:, 0:shape[2]].unsqueeze(1).to_broadcast(shape),
                                       numbers[:, lo:hi].unsqueeze(2).to_broadcast(shape), ALU.is_equal)

            def hot_lanes(lo, hi):
                one_hots(hot_lane, slot_h, lo, hi).then_inc(hot, hi - lo)

            V.tensor_copy(slot_h[:, :], slot_p[:, 1, :])
            link(V.tensor_tensor(beyond[:, :, :], slot_p[:, 0, :].unsqueeze(1).to_broadcast(pairs),
                                 run_end[:, :].unsqueeze(2).to_broadcast(pairs), ALU.is_ge))
            V.tensor_tensor(beyond[:, :, :], beyond[:, :, :], run_step[:, :].unsqueeze(2).to_broadcast(pairs),
                            ALU.mult).then_inc(pos_step, 1)
            hot_lanes(0, GROUP)
            dve.wait_ge(pos_step, 1)
            V.tensor_reduce(moved[:, :], beyond[:, :, :].rearrange("p k m -> p m k"), AX.X, ALU.add).then_inc(pos_step, 1)
            dve.wait_ge(pos_step, 2)
            V.scalar_tensor_tensor(out=step_h[:, :], in0=slot_p[:, 0, :], scalar=float(SLOTS), in1=moved[:, :],
                                   op0=ALU.mult, op1=ALU.add).then_inc(steps_known, 1)
            dve.wait_ge(steps_known, 1)
            one_hots(hot_tile, step_h, 0, GROUP).then_inc(hot_own, 1)
            for lo in range(GROUP, K * NT, GROUP):
                one_hots(hot_tile, step_h, lo, lo + GROUP).then_inc(hot_own, 1)
                if lo == GROUP:
                    hot_lanes(lo, lo + GROUP)
            for lo in range(2 * GROUP, K * NT, GROUP // 2):
                hot_lanes(lo, lo + GROUP // 2)
            dve.wait_ge(inv_mm, 1)
            V.tensor_scalar(inv[:, 0, :], ps_inv, 0.0, float(TOKENS), ALU.is_lt, ALU.mult)
            link(V.tensor_scalar(inv[:, 1, :], ps_inv, -1.0, None, ALU.mult))
            link(V.tensor_tensor(inv[:, 1, :], inv[:, 1, :], ps_inv, ALU.max))
            V.tensor_scalar(token_of[:, 0:ST], inv[:, 1, :], -1.0, 0.0, ALU.add, ALU.max).then_inc(tokens_known, 1)
            V.tensor_scalar(inv[:, 2, :], inv[:, 1, :], 0.5, None, ALU.is_gt)
            link(V.tensor_tensor(inv[:, 3, :], inv[:, 1, :], inv[:, 0, :], ALU.add))
            spare = dump[:, :, :].rearrange("p a b -> p (a b)")
            link(V.scalar_tensor_tensor(out=inv[:, 3, :], in0=inv[:, 3, :], scalar=-1.0, in1=spare,
                                        op0=ALU.add, op1=ALU.subtract))
            link(V.tensor_tensor(inv[:, 3, :], inv[:, 3, :], inv[:, 2, :], ALU.mult))
            V.tensor_tensor(dest_of[:, :], inv[:, 3, :], spare, ALU.add).then_inc(routed, 1)
            for k, (group, gw) in enumerate(((first[:, :, 0, :], pmax[:, :, 0]), (second[:, :, :], gmax2[:, :]))):
                link(V.tensor_tensor(wg_[:, :, :], group, pmax[:, :, 1:C], ALU.mult))
                link(V.tensor_reduce(wk[:, k, :], wg_[:, :, :], AX.X, ALU.add))
                link(V.tensor_tensor(wk[:, k, :], wk[:, k, :], gw, ALU.mult))
            for k in range(K):
                V.tensor_tensor(placed[:, k, :, :], sel[:, k, :, :],
                                wk[:, k, :].unsqueeze(2).to_broadcast([P, NT, EX]), ALU.mult)
            link(V.tensor_copy(wsel[:, :, :], sel[:, 0, :, :]))
            link(V.tensor_tensor(mixw[:, :, D:D + EX], placed[:, 0, :, :], placed[:, 1, :, :], ALU.add))

            def turned(t, v):
                dve.wait_ge(xs_mm, t + 1)
                at_least(dve, up_mm, t - 1)
                V.tensor_copy(xs_m[v][:, :], pX[v][:, 0:P])
                V.tensor_copy(xs_r[v][:, :], pX[v][0:DR + 1, P:2 * P]).then_inc(xs_ev, 1)

            turned(0, 0)
            turned(1, 1)

            def body(t, u, i):
                v = u % 2
                turned(t + 2, v)
                dve.wait_ge(down_mm, t + 1)
                at_least(dve, sent[u], 16 * i)
                V.tensor_copy(yo[u][:, :], pY[v][:, 0:D]).then_inc(y_ev, 1)

            for u in range(SLOTS):
                body(u, u, 0)
            with dve.Fori(1, FULL) as i:
                for u in range(SLOTS):
                    body(i * SLOTS + u, u, i)
            used = tiles_in_use(dve)
            with dve.Fori(FULL, ROUNDS) as i:
                for u in range(SLOTS):
                    with dve.If(used > i * SLOTS + u):
                        body(i * SLOTS + u, u, i)

            dve.wait_ge(resid, 1)

            def mix(i):
                dve.wait_ge(y1w, i + 1)
                V.scalar_tensor_tensor(out=mixw[:, i, 0:D], in0=ys[:, 1, i, :], scalar=wk[:, 1, i:i + 1],
                                       in1=ys[:, 0, i, :], op0=ALU.mult, op1=ALU.add).then_inc(mix_done, 1)

            for i in range(2 * CB):
                mix(i)
            for b in range(B):
                for c in range(CB):
                    dve.wait_ge(proj_mm, CB * b + c + 1)
                    ins = V.bn_stats(stats[:, 0, c, :], ps_y[b % 3][c])
                link(ins)
                for c in range(CB):
                    ins = V.bn_aggr(mv[:, 2, c, :], stats[:, 0, c, :])
                link(ins)
                root_input(2, var3)
                if b + 2 < B:
                    mix(CB * (b + 2))
                dve.wait_ge(sd3, b + 1)
                V.reciprocal(rs[:, 2, :], sd[:, 2, :]).then_inc(root_step, 1)
                if b + 2 < B:
                    mix(CB * (b + 2) + 1)
                dve.wait_ge(root_step, 3 * b + 1)
                newton(2).then_inc(root_step, 1)
                dve.wait_ge(root_step, 3 * b + 2)
                V.reciprocal(rs[:, 2, :], tn[:, 2, :]).then_inc(root_step, 1)
                dve.wait_ge(root_step, 3 * b + 3)
                V.scalar_tensor_tensor(out=nm[:, :], in0=mv[:, 2, :, 0], scalar=-1.0, in1=rs[:, 2, :],
                                       op0=ALU.mult, op1=ALU.mult).then_inc(norm3, 1)
            tiles = slice(NT - CB, NT)
            dve.wait_ge(z_done, NT)
            link(V.tensor_tensor(fin[:, tiles, :], fin[:, tiles, :], gam[:, :].unsqueeze(1).to_broadcast([P, CB, D]), ALU.mult))
            dve.wait_ge(fin_done, B - 1)
            V.tensor_tensor(fin[:, tiles, :], fin[:, tiles, :], h2[:, tiles, :], ALU.add).then_inc(fin_done, 1)

        @block.tensor
        def _(pe):
            def two(out_ap, m_l, m_r, r_l, r_r):
                pe.matmul(out_ap, m_l, r_l, start=True, stop=False)
                return pe.matmul(out_ap, m_r, r_r, start=False, stop=True)

            pe.wait_ge(masks, 2)
            half = ident[0:D // 2, 0:D // 2]
            pe.wait_ge(proj_twice, 1)
            for a in range(2):
                mm = pe.transpose(ps_pr[:, a * D // 2:(a + 1) * D // 2],
                                  proj_s[:, a, :, :].rearrange("p c r -> p (c r)"), half)
            mm.then_inc(projT_mm, 1)
            for a in range(2):
                mm = pe.matmul(ps_mean, mean_w[:, :], proj_s[:, a, 0, :], start=(a == 0), stop=(a == 1))
            mm.then_inc(mean_mm, 1)

            def turn_weights():
                pe.wait_ge(vkq_in, 112)
                pe.wait_ge(PcT_done, 1)
                for m in range(3):
                    for c in range(2):
                        for a in range(2):
                            mm = pe.transpose(ps_w[m][:, c, a * D // 2:(a + 1) * D // 2], vkq[:, m, a, c:D:2], half)
                    mm.then_inc(vkqT_mm, 1)
                pe.wait_ge(gate_in, 48)
                pe.wait_ge(Pc_done, 1)
                for a in range(2):
                    mm = pe.matmul(ps_gmean, mean_w[:, :], gates[:, a, :, :].rearrange("p c e -> p (c e)"),
                                   start=(a == 0), stop=(a == 1))
                mm.then_inc(gmean_mm, 1)

            def halves(out_ap, lhsT, rhs):
                for c in range(2):
                    mm = pe.matmul(out_ap, lhsT(c), rhs(c), start=(c == 0), stop=(c == 1))
                return mm

            def products_of_weights():
                pe.wait_ge(Pc_done, 1)
                pe.wait_ge(vkqT_ev, 3)
                halves(ps_m2, lambda c: Pc[:, c, :], lambda c: vkqT[:, 0, c, :]).then_inc(M2_mm, 1)
                for m in range(3):
                    for a in range(2):
                        mm = halves(ps_vkqc[:, m, a, :], lambda c: vkqT[:, m, c, a * D // 2:(a + 1) * D // 2],
                                    lambda c: Pc[:, c, :])
                mm.then_inc(kq_mm, 1)
                pe.wait_ge(kq_ev, 1)
                pe.wait_ge(kq_bias, 1)
                halves(ps_m1, lambda a: vkqc[:, 1, a, :], lambda a: vkqc[:, 2, a, :]).then_inc(M1_mm, 1)
                pe.wait_ge(gates_done, 1)
                halves(ps_M2g, lambda a: vkqc[:, 0, a, :], lambda a: gates_c[:, a, :])
                halves(ps_PTg, lambda a: proj_s[:, a, :, :].rearrange("p c r -> p (c r)"),
                       lambda a: gates_c[:, a, :]).then_inc(gates_mm, 1)

            def low_turn(b):
                pe.wait_ge(gathered[b], 16 * CB)
                at_least(pe, low_ev, b)
                pe.transpose(ps_low, emb[:, CB * b:CB * b + CB, :].rearrange("p c r -> p (c r)"),
                             ident[:, :]).then_inc(low_mm, 1)

            low_turn(0)
            for s in range(STEPS):
                if stage(s, 2):
                    b = s - 2
                    q = b % 2
                    if b == 0:
                        pe.wait_ge(vkqT_ev, 1)
                    pe.wait_ge(l_done, b + 1)
                    at_least(pe, gram_ev, b)
                    at_least(pe, gv_ev, b)
                    for c in range(CB):
                        mm = pe.matmul(ps_g, lh[:, q, c, :], lh[:, q, c, :], start=(c == 0), stop=(c == CB - 1))
                    mm.then_inc(gram_mm, 1)
                    at_least(pe, lT_ev, b)
                    for c in range(CB):
                        mm = pe.transpose(ps_lT[:, c * P:(c + 1) * P], lh[:, q, c, :], ident[:, :])
                    mm.then_inc(lT_mm, 1)
                if stage(s, 0) and s > 0:
                    low_turn(s)
                if s == 3:
                    pe.wait_ge(PT_done, 2 * CB)
                if stage(s, 3):
                    b = s - 3
                    q = b % 2
                    pe.wait_ge(bb_ev, b + 1)
                    pe.wait_ge(lT_ev, b + 1)
                    at_least(pe, h2_ev, b)
                    for c in range(CB):
                        pe.matmul(ps_o[:, c, :], lowT[:, b, :], PT[:, c, :], start=True, stop=False)
                        mm = pe.matmul(ps_o[:, c, :], lT[:, q, c * P:(c + 1) * P], bb[:, q, :], start=False, stop=True)
                    mm.then_inc(att_mm, 1)
                if stage(s, 2):
                    b = s - 2
                    if b == 0:
                        pe.wait_ge(M2_ev, 2)
                        pe.wait_ge(M1_ev, 1)
                    pe.wait_ge(gram_ev, b + 1)
                    pe.matmul(ps_v, gram[:, b % 2, :], M2[:, :], start=True, stop=True).then_inc(gv_mm, 1)
                if stage(s, 0):
                    b = s
                    pe.wait_ge(low_ev, b + 1)
                    if b == 0:
                        pe.wait_ge(PcT_done, 1)
                    at_least(pe, h_read, b)
                    pe.matmul(ps_hc, lowT[:, b, :], PcT[:, :, :], start=True, stop=True).then_inc(h_mm, 1)
                if s == 0:
                    turn_weights()
                if s == 1:
                    products_of_weights()
                if stage(s, 2):
                    b = s - 2
                    pe.wait_ge(gv_ev, b + 1)
                    pe.matmul(ps_b, M1T[:, :], gv[:, b % 2, :], start=True, stop=True).then_inc(bb_mm, 1)

            pe.wait_ge(b2_in, 48)
            pe.wait_ge(h2_ev, B)
            pe.transpose(ps_2m, b2_s[:, 0:P], ident[0:EX, 0:EX])
            pe.transpose(ps_2r, b2_s[:, P:D], ident[0:EX, 0:EX]).then_inc(b2T_mm, 1)
            pe.wait_ge(b2T_ev, 1)
            two(ps_2p, b2T_m[:, :], b2T_r[:, :], Wp_m[:, :], Wp_r[0:DR, :]).then_inc(b2p_mm, 1)

            pe.wait_ge(picked, 1)
            chosen = both[:, :, :].rearrange("p i e -> p (i e)")
            pe.matmul(ps_rank.rearrange("p i e -> p (i e)"), before[:, :], chosen, start=True, stop=True)
            pe.matmul(ps_tot, ones[:, :], both[:, :, :].rearrange("p i e -> p e i"), start=True, stop=True).then_inc(counted, 1)
            pe.wait_ge(b2p_ev, 1)
            pe.wait_ge(experts_counted, 1)
            pe.transpose(ps_expert_row, expert_f[:, :], ident[:, :]).then_inc(experts_mm, 1)
            for m in range(K * NT):
                pe.wait_ge(hot, (m // (GROUP // 2) + 1) * (GROUP // 2) if m >= 2 * GROUP else (m // GROUP + 1) * GROUP)
                pe.wait_ge(hot_row, m // GROUP + 1)
                mm = pe.matmul(ps_inv, hot_lane[:, m, :], hot_tile[:, m, :], start=(m == 0), stop=(m == K * NT - 1))
            mm.then_inc(inv_mm, 1)

            def keep_busy(scratch):
                for _ in range(BUSY):
                    pe.matmul(scratch, ident[:, :], ident[:, :], start=True, stop=True)

            keep_busy(pA[1][:, 0:P])

            def turn(t, u, loads):
                v = u % 2
                pe.wait_ge(tok_in[u], loads)
                at_least(pe, xs_ev, t - 1)
                pe.transpose(pX[v][:, 0:P], xg[u][:, 0:P], ident[:, :])
                pe.transpose(pX[v][0:DR + 1, P:2 * P], xg[u][:, P:D1], ident[:, :]).then_inc(xs_mm, 1)

            def up(t, u, loads):
                v = u % 2
                pe.wait_ge(xs_ev, t + 1)
                pe.wait_ge(w_in[u], loads)
                at_least(pe, gelu_done, t - 1)
                for j in range(HC):
                    mm = two(pA[v][:, j * P:(j + 1) * P], W1_m[u][:, j::HC], W1_r[u][:, j::HC], xs_m[v][:, :], xs_r[v][:, :])
                mm.then_inc(up_mm, 1)

            def down(t, u):
                v = u % 2
                pe.wait_ge(gelu_done, t + 1)
                at_least(pe, y_ev, t - 1)
                for j in range(HC):
                    mm = pe.matmul(pY[v][:, 0:D], hT[v][:, j * P:(j + 1) * P], W2_s[u][:, j, :],
                                   start=(j == 0), stop=(j == HC - 1))
                mm.then_inc(down_mm, 1)

            turn(0, 0, 16)
            up(0, 0, 64)
            turn(1, 1, 16)

            def next_up(t, u, i):
                up(t + 1, (u + 1) % SLOTS, 64 * (i + (2 if u == SLOTS - 1 else 1)))

            def next_turn(t, u, i):
                turn(t + 2, (u + 2) % SLOTS, 16 * (i + (2 if u >= SLOTS - 2 else 1)))

            def body(t, u, i):
                next_turn(t, u, i)
                next_up(t, u, i)
                down(t, u)

            for u in range(SLOTS):
                body(u, u, 0)
            with pe.Fori(1, FULL) as i:
                for u in range(SLOTS):
                    body(i * SLOTS + u, u, i)
            used = tiles_in_use(pe)
            with pe.Fori(FULL, ROUNDS) as i:
                for u in range(SLOTS):
                    with pe.If(used > i * SLOTS + u):
                        next_turn(i * SLOTS + u, u, i)
                        with pe.If(used > i * SLOTS + u + 1):
                            next_up(i * SLOTS + u, u, i)
                        down(i * SLOTS + u, u)

            pe.wait_ge(moe_done, 1)
            keep_busy(pA[1][:, 0:P])
            for i in range(NT + 1):
                if i < NT:
                    pe.wait_ge(mix_done, i + 1)
                    at_least(pe, mixT_ev, i - 1)
                    pe.transpose(pX[i % 2][:, 0:P], mixw[:, i, 0:P], ident[:, :])
                    pe.transpose(pX[i % 2][0:DR + EX + 1, P:2 * P], mixw[:, i, P:D + EX + 1], ident[:, :]).then_inc(mixT_mm, 1)
                if i >= 1:
                    j = i - 1
                    if j == 0:
                        pe.wait_ge(b2p_in, 16)
                        pe.wait_ge(tail_in, 48)
                    pe.wait_ge(mixT_ev, j + 1)
                    at_least(pe, z_done, CB * (j // CB - 2))
                    two(ps_y[j // CB % 3][j % CB], mixT_m[:, j % 2, :], mixT_r[:, j % 2, :], Wp_m[:, :], Wp_r[:, :]).then_inc(proj_mm, 1)


_INS = ["x", "L0_tok_embed_table", "L0_tok_proj_up", "L0_attn_Wq", "L0_attn_bq", "L0_attn_Wk", "L0_attn_bk", "L0_attn_Wv",
        "L0_attn_bv", "L0_ffn_Wg", "L0_ffn_bg", "L0_ffn_We", "L0_ffn_be", "L0_ffn_W1", "L0_ffn_b1", "L0_ffn_W2",
        "L0_ffn_b2", "L0_ffn_Wp", "L0_ffn_bp", "L0_ffn_gamma", "L0_ffn_beta"]


def kernel(**inputs):
    import concourse.bacc as _bacc
    from concourse.bass_utils import run_bass_kernel_spmd as _run

    nc = _bacc.Bacc("TRN2", target_bir_lowering=False, num_devices=1)
    arrays, args = {}, []
    for name in _INS:
        a = np.ascontiguousarray(inputs[name])
        arrays[f"in_{name}_dram"] = a
        args.append(nc.dram_tensor(f"in_{name}_dram", a.shape, mybir.dt.from_np(a.dtype), kind="ExternalInput").ap())
    shape = (*inputs["x"].shape, inputs["L0_tok_proj_up"].shape[0])
    out = nc.dram_tensor("out_0_dram", shape, F32, kind="ExternalOutput").ap()
    lm_tower(nc, *args, out)
    r = _run(nc, [arrays], core_ids=[0])
    return r.results[0]["out_0_dram"]
```
